# Optimizing a Trainium2 kernel written in Bass

```python
import numpy as np
import jax
import jax.numpy as jnp

def _softmax(x, axis=-1):
    return jax.nn.softmax(x, axis=axis)

def _gelu(x):
    return jax.nn.gelu(x, approximate=True)

def _silu(x):
    return jax.nn.silu(x)

def _sigmoid(x):
    return jax.nn.sigmoid(x)

def _layernorm(x, axis=-1, eps=1e-05):
    m = jnp.mean(x, axis=axis, keepdims=True)
    v = jnp.var(x, axis=axis, keepdims=True)
    return (x - m) / jnp.sqrt(v + eps)

def _scatter_add(tgt, idx, src, axis=0):
    return tgt.at[idx].add(src)

def _segment_sum(src, seg, n):
    return jax.ops.segment_sum(src, seg, n)
kernel_name = 'mk_lm_tower_d1_tok_ids4096_r4_ade688'

def setup_inputs(seed: int=0):
    np.random.seed(seed)
    _w = jnp.asarray

    def _rec_inputs():
        import jax
        import jax.numpy as jnp
        _rk = jax.random.key(seed)
        x = jax.random.randint(jax.random.fold_in(_rk, 1), (16, 512), 0, 1024, jnp.int32)
        return x
    x = _rec_inputs()

    def _L0_tok_setup():
        import jax, jax.numpy as jnp
        import numpy as np
        V = 1024
        M = 4
        B = 8
        L = 512

        def _contexts(idx, vocab, order):
            Bb, Ll = idx.shape
            cols = []
            for k in range(order):
                s = order - 1 - k
                if s == 0:
                    cols.append(idx)
                else:
                    pad = jnp.full((Bb, s), vocab, dtype=idx.dtype)
                    cols.append(jnp.concatenate([pad, idx[:, :Ll - s]], axis=1))
            return jnp.stack(cols, axis=-1)
        key = jax.random.key(seed)
        k1, k2 = jax.random.split(key, 2)
        idx = jax.random.randint(k1, (B, L), 0, V, dtype=jnp.int64 if jax.config.jax_enable_x64 else jnp.int32)
        fan_in = M * (V + 1)
        bound = 1.0 / np.sqrt(fan_in)
        W = jax.random.uniform(k2, (V, fan_in), minval=-bound, maxval=bound, dtype=jnp.float32)
        b = jax.random.uniform(jax.random.fold_in(k2, 1), (V,), minval=-bound, maxval=bound, dtype=jnp.float32)
        return {'idx': idx, 'W': W, 'b': b}
    _L0_tok_all = _L0_tok_setup()
    _L0_tok_in = {k: v for k, v in _L0_tok_all.items() if k in ('W', 'b')}
    del _L0_tok_all

    def _L0_attn_setup():
        import jax, jax.numpy as jnp
        import numpy as np
        DEPTH, DIM, DFF, VOCAB = (4, 128, 512, 1024)
        EPS = 1e-05

        def layernorm(x, w, b):
            mu = jnp.mean(x, axis=-1, keepdims=True)
            var = jnp.mean((x - mu) ** 2, axis=-1, keepdims=True)
            return (x - mu) * jax.lax.rsqrt(var + EPS) * w + b

        def sconv(x, phazor_c, last_conv_c):
            B, L, D = x.shape
            r = jnp.abs(phazor_c)
            p = jnp.tanh(r) * jnp.exp(1j * jnp.angle(phazor_c))
            prog = p[None, :] ** jnp.arange(L, dtype=jnp.float32)[:, None]
            filt_fft = jnp.fft.fft(prog, n=2 * L, axis=0)
            x_fft = jnp.fft.fft(x.astype(jnp.complex64), n=2 * L, axis=1)
            conv = jnp.fft.ifft(filt_fft[None] * x_fft, axis=1)[:, :L]
            conv = conv + last_conv_c[None, None, :] * prog[None] * p[None, None, :]
            return conv.real.astype(x.dtype)

        def _forward(x, Win, bin, ln1_w, ln1_b, phz_re, phz_im, lc_re, lc_im, sc_lin, ln2_w, ln2_b, W1, b1, W2, b2, lnl_w, lnl_b, Wout, bout):
            h = jnp.einsum('blv,dv->bld', x, Win) + bin

            def body(h, p):
                l1w, l1b, pr, pi, lr, li, scl, l2w, l2b, w1, b1_, w2, b2_ = p
                y = jax.nn.silu(layernorm(h, l1w, l1b))
                y = sconv(y, pr + 1j * pi, lr + 1j * li)
                h = h + y * scl
                y = layernorm(h, l2w, l2b)
                y = jax.nn.silu(jnp.einsum('bld,fd->blf', y, w1) + b1_)
                y = jnp.einsum('blf,df->bld', y, w2) + b2_
                return (h + y, None)
            xs = (ln1_w, ln1_b, phz_re, phz_im, lc_re, lc_im, sc_lin, ln2_w, ln2_b, W1, b1, W2, b2)
            h, _ = jax.lax.scan(body, h, xs)
            h = layernorm(h, lnl_w, lnl_b)
            return jnp.einsum('bld,vd->blv', h, Wout) + bout
        key = jax.random.key(seed)
        ks = jax.random.split(key, 20)
        f32 = jnp.float32
        inp = {}
        inp['x'] = jax.random.normal(ks[0], (2, 1024, VOCAB), dtype=f32)
        inp['Win'] = jax.random.normal(ks[1], (DIM, VOCAB), dtype=f32) * VOCAB ** (-0.5)
        inp['bin'] = jnp.zeros((DIM,), f32)
        inp['ln1_w'] = jnp.ones((DEPTH, DIM), f32)
        inp['ln1_b'] = jnp.zeros((DEPTH, DIM), f32)
        ang = 2 * np.pi * jnp.arange(DIM, dtype=f32) / DIM
        mag = jnp.abs(jax.random.normal(ks[2], (DEPTH, DIM), dtype=f32))
        inp['phz_re'] = mag * jnp.cos(ang)[None]
        inp['phz_im'] = mag * jnp.sin(ang)[None]
        inp['lc_re'] = jax.random.normal(ks[3], (DEPTH, DIM), dtype=f32)
        inp['lc_im'] = jax.random.normal(ks[4], (DEPTH, DIM), dtype=f32)
        inp['sc_lin'] = jnp.ones((DEPTH, DIM), f32)
        inp['ln2_w'] = jnp.ones((DEPTH, DIM), f32)
        inp['ln2_b'] = jnp.zeros((DEPTH, DIM), f32)
        inp['W1'] = jax.random.normal(ks[5], (DEPTH, DFF, DIM), dtype=f32) * DIM ** (-0.5)
        inp['b1'] = jnp.zeros((DEPTH, DFF), f32)
        inp['W2'] = jax.random.normal(ks[6], (DEPTH, DIM, DFF), dtype=f32) * DFF ** (-0.5)
        inp['b2'] = jnp.zeros((DEPTH, DIM), f32)
        inp['lnl_w'] = jnp.ones((DIM,), f32)
        inp['lnl_b'] = jnp.zeros((DIM,), f32)
        inp['Wout'] = jax.random.normal(ks[7], (VOCAB, DIM), dtype=f32) * DIM ** (-0.5)
        inp['bout'] = jnp.zeros((VOCAB,), f32)
        return inp
    _L0_attn_all = _L0_attn_setup()
    _L0_attn_in = {k: v for k, v in _L0_attn_all.items() if k in ('Win', 'bin', 'ln1_w', 'ln1_b', 'phz_re', 'phz_im', 'lc_re', 'lc_im', 'sc_lin', 'ln2_w', 'ln2_b', 'W1', 'b1', 'W2', 'b2', 'lnl_w', 'lnl_b', 'Wout', 'bout')}
    del _L0_attn_all

    def _L0_ffn_setup():
        import jax, jax.numpy as jnp
        import numpy as np
        key = jax.random.key(seed)
        k = jax.random.split(key, 6)
        x = jax.random.normal(k[0], (4, 512, 1024), jnp.float32)
        W = jax.random.normal(k[1], (1024, 1024), jnp.float32) * 0.02
        bias = jax.random.normal(k[2], (1024,), jnp.float32) * 0.02
        A = jax.random.normal(k[3], (16, 16, 1024), jnp.float32) * 0.02
        Bf = jax.random.normal(k[4], (16, 1024, 16), jnp.float32) * 0.02
        coeffs = jax.random.uniform(k[5], (16,), jnp.float32)
        scales = jnp.full((16,), 0.5, jnp.float32)
        return {'x': x, 'W': W, 'bias': bias, 'A': A, 'Bf': Bf, 'coeffs': coeffs, 'scales': scales}
    _L0_ffn_all = _L0_ffn_setup()
    _L0_ffn_in = {k: v for k, v in _L0_ffn_all.items() if k in ('W', 'bias', 'A', 'Bf', 'coeffs', 'scales')}
    del _L0_ffn_all
    return {'x': x, 'L0_tok_W': _L0_tok_in['W'], 'L0_tok_b': _L0_tok_in['b'], 'L0_attn_Win': _L0_attn_in['Win'], 'L0_attn_bin': _L0_attn_in['bin'], 'L0_attn_ln1_w': _L0_attn_in['ln1_w'], 'L0_attn_ln1_b': _L0_attn_in['ln1_b'], 'L0_attn_phz_re': _L0_attn_in['phz_re'], 'L0_attn_phz_im': _L0_attn_in['phz_im'], 'L0_attn_lc_re': _L0_attn_in['lc_re'], 'L0_attn_lc_im': _L0_attn_in['lc_im'], 'L0_attn_sc_lin': _L0_attn_in['sc_lin'], 'L0_attn_ln2_w': _L0_attn_in['ln2_w'], 'L0_attn_ln2_b': _L0_attn_in['ln2_b'], 'L0_attn_W1': _L0_attn_in['W1'], 'L0_attn_b1': _L0_attn_in['b1'], 'L0_attn_W2': _L0_attn_in['W2'], 'L0_attn_b2': _L0_attn_in['b2'], 'L0_attn_lnl_w': _L0_attn_in['lnl_w'], 'L0_attn_lnl_b': _L0_attn_in['lnl_b'], 'L0_attn_Wout': _L0_attn_in['Wout'], 'L0_attn_bout': _L0_attn_in['bout'], 'L0_ffn_W': _L0_ffn_in['W'], 'L0_ffn_bias': _L0_ffn_in['bias'], 'L0_ffn_A': _L0_ffn_in['A'], 'L0_ffn_Bf': _L0_ffn_in['Bf'], 'L0_ffn_coeffs': _L0_ffn_in['coeffs'], 'L0_ffn_scales': _L0_ffn_in['scales']}

def reference(x, L0_tok_W, L0_tok_b, L0_attn_Win, L0_attn_bin, L0_attn_ln1_w, L0_attn_ln1_b, L0_attn_phz_re, L0_attn_phz_im, L0_attn_lc_re, L0_attn_lc_im, L0_attn_sc_lin, L0_attn_ln2_w, L0_attn_ln2_b, L0_attn_W1, L0_attn_b1, L0_attn_W2, L0_attn_b2, L0_attn_lnl_w, L0_attn_lnl_b, L0_attn_Wout, L0_attn_bout, L0_ffn_W, L0_ffn_bias, L0_ffn_A, L0_ffn_Bf, L0_ffn_coeffs, L0_ffn_scales):
    import jax
    import jax.numpy as jnp

    def _L0_tok_ref(idx, W, b):
        import jax, jax.numpy as jnp
        import numpy as np
        V = 1024
        M = 4
        B = 8
        L = 512

        def _contexts(idx, vocab, order):
            Bb, Ll = idx.shape
            cols = []
            for k in range(order):
                s = order - 1 - k
                if s == 0:
                    cols.append(idx)
                else:
                    pad = jnp.full((Bb, s), vocab, dtype=idx.dtype)
                    cols.append(jnp.concatenate([pad, idx[:, :Ll - s]], axis=1))
            return jnp.stack(cols, axis=-1)
        vocab = W.shape[0]
        order = W.shape[1] // (vocab + 1)
        x = _contexts(idx, vocab, order)
        Wt = W.T.reshape(order, vocab + 1, vocab)
        logits = b
        for k in range(order):
            logits = logits + Wt[k][x[..., k]]
        return logits

    def _L0_attn_ref(x, Win, bin, ln1_w, ln1_b, phz_re, phz_im, lc_re, lc_im, sc_lin, ln2_w, ln2_b, W1, b1, W2, b2, lnl_w, lnl_b, Wout, bout):
        import jax, jax.numpy as jnp
        import numpy as np
        DEPTH, DIM, DFF, VOCAB = (4, 128, 512, 1024)
        EPS = 1e-05

        def layernorm(x, w, b):
            mu = jnp.mean(x, axis=-1, keepdims=True)
            var = jnp.mean((x - mu) ** 2, axis=-1, keepdims=True)
            return (x - mu) * jax.lax.rsqrt(var + EPS) * w + b

        def sconv(x, phazor_c, last_conv_c):
            B, L, D = x.shape
            r = jnp.abs(phazor_c)
            p = jnp.tanh(r) * jnp.exp(1j * jnp.angle(phazor_c))
            prog = p[None, :] ** jnp.arange(L, dtype=jnp.float32)[:, None]
            filt_fft = jnp.fft.fft(prog, n=2 * L, axis=0)
            x_fft = jnp.fft.fft(x.astype(jnp.complex64), n=2 * L, axis=1)
            conv = jnp.fft.ifft(filt_fft[None] * x_fft, axis=1)[:, :L]
            conv = conv + last_conv_c[None, None, :] * prog[None] * p[None, None, :]
            return conv.real.astype(x.dtype)

        def _forward(x, Win, bin, ln1_w, ln1_b, phz_re, phz_im, lc_re, lc_im, sc_lin, ln2_w, ln2_b, W1, b1, W2, b2, lnl_w, lnl_b, Wout, bout):
            h = jnp.einsum('blv,dv->bld', x, Win) + bin

            def body(h, p):
                l1w, l1b, pr, pi, lr, li, scl, l2w, l2b, w1, b1_, w2, b2_ = p
                y = jax.nn.silu(layernorm(h, l1w, l1b))
                y = sconv(y, pr + 1j * pi, lr + 1j * li)
                h = h + y * scl
                y = layernorm(h, l2w, l2b)
                y = jax.nn.silu(jnp.einsum('bld,fd->blf', y, w1) + b1_)
                y = jnp.einsum('blf,df->bld', y, w2) + b2_
                return (h + y, None)
            xs = (ln1_w, ln1_b, phz_re, phz_im, lc_re, lc_im, sc_lin, ln2_w, ln2_b, W1, b1, W2, b2)
            h, _ = jax.lax.scan(body, h, xs)
            h = layernorm(h, lnl_w, lnl_b)
            return jnp.einsum('bld,vd->blv', h, Wout) + bout
        return _forward(x, Win, bin, ln1_w, ln1_b, phz_re, phz_im, lc_re, lc_im, sc_lin, ln2_w, ln2_b, W1, b1, W2, b2, lnl_w, lnl_b, Wout, bout)

    def _L0_ffn_ref(x, W, bias, A, Bf, coeffs, scales):
        import jax, jax.numpy as jnp
        import numpy as np
        out = jnp.einsum('bsd,od->bso', x, W) + bias
        xa = jnp.einsum('bsd,erd->ebsr', x, A)
        w = coeffs * scales
        upd = jnp.einsum('ebsr,eor,e->bso', xa, Bf, w)
        return out + upd
    h = _L0_tok_ref(x, L0_tok_W, L0_tok_b)
    h = h + _L0_attn_ref(_layernorm(h, axis=-1), L0_attn_Win, L0_attn_bin, L0_attn_ln1_w, L0_attn_ln1_b, L0_attn_phz_re, L0_attn_phz_im, L0_attn_lc_re, L0_attn_lc_im, L0_attn_sc_lin, L0_attn_ln2_w, L0_attn_ln2_b, L0_attn_W1, L0_attn_b1, L0_attn_W2, L0_attn_b2, L0_attn_lnl_w, L0_attn_lnl_b, L0_attn_Wout, L0_attn_bout)
    h = h + _L0_ffn_ref(_layernorm(h, axis=-1), L0_ffn_W, L0_ffn_bias, L0_ffn_A, L0_ffn_Bf, L0_ffn_coeffs, L0_ffn_scales)
    return h

_drawn_inputs = setup_inputs


def setup_inputs(seed=0):
    import zlib

    import numpy as np

    out = dict(_drawn_inputs(seed))
    spreads = {'L0_attn_bin': (0.0, 0.1),
     'L0_attn_ln1_w': (1.0, 0.2),
     'L0_attn_ln1_b': (0.0, 0.1),
     'L0_attn_sc_lin': (1.0, 0.2),
     'L0_attn_ln2_w': (1.0, 0.2),
     'L0_attn_ln2_b': (0.0, 0.1),
     'L0_attn_b1': (0.0, 0.1),
     'L0_attn_b2': (0.0, 0.1),
     'L0_attn_lnl_w': (1.0, 0.2),
     'L0_attn_lnl_b': (0.0, 0.1),
     'L0_attn_bout': (0.0, 0.1),
     'L0_ffn_scales': (0.5, 0.6)}
    factors = {'L0_ffn_bias': 3.469, 'L0_ffn_coeffs': 2.786}
    for name, (base, spread) in spreads.items():
        noise = np.random.default_rng([zlib.crc32(name.encode()), seed]).standard_normal(out[name].shape)
        drawn = base * np.exp(spread * noise) if base else spread * noise
        out[name] = jnp.asarray(drawn.astype(out[name].dtype))
    for name, factor in factors.items():
        out[name] = (out[name] * factor).astype(out[name].dtype)
    return out
```

```python
import concourse.bass as bass
from concourse import mybir
from contextlib import ExitStack

P = 128
ABSMAX = bass.bass_isa.ReduceOp.absmax
VOCAB, DIM, DFF, DEPTH = 1024, 128, 512, 4
NSEQ, SEQ = 16, 512
ORDER = 4
EXP = 16 * 16
TILES = NSEQ * SEQ // P
TPS = SEQ // P
STEPS = 2 * TPS
ROUNDS = NSEQ // 2
ROWS = ORDER * (VOCAB + 1)
EPS = 1e-5
ZUP = 256.0
WUP = 4096.0
PCOLS = {}
_at = 0
for _n, _w in (("ln1_w", 4), ("ln1_b", 4), ("phz_re", 4), ("phz_im", 4), ("lc_re", 4), ("lc_im", 4),
               ("sc_lin", 4), ("ln2_w", 4), ("ln2_b", 4), ("b2", 4), ("b1", 16), ("lnl_w", 1),
               ("lnl_b", 1), ("tok_b", 8), ("coeffs", 2), ("scales", 2)):
    PCOLS[_n] = (_at, _w)
    _at += _w
PWIDTH = _at


def program(nc, idx, tok_wt, tok_w, cols, tok_b, win, bin_, w1t, w2t, woutt, bout, ffn_wt, ffn_bias,
            lora_a, lora_bt, out, ptab):
    f32, f16, bf16, i32 = mybir.dt.float32, mybir.dt.float16, mybir.dt.bfloat16, mybir.dt.int32
    u32 = mybir.dt.uint32
    ALU, ACT, AX = mybir.AluOpType, mybir.ActivationFunctionType, mybir.AxisListType
    HV = VOCAB // 2
    VC = VOCAB // P
    FC = DFF // P
    KC = EXP // P

    ctx = ExitStack()
    with ctx:
        def sb(name, shape, dt=f32):
            return ctx.enter_context(nc.sbuf_tensor(name, shape, dt))

        def pb(name, shape, dt=f32):
            return ctx.enter_context(nc.psum_tensor(name, shape, dt))

        def sem(name):
            return ctx.enter_context(nc.semaphore(name))

        ident = sb("ident", [P, P])
        ident16 = sb("ident16", [P, P], f16)
        ones_b = sb("ones_b", [P, P], bf16)
        par = sb("par", [P, PWIDTH])
        idx_sb = sb("idx_sb", [P, TILES, ORDER], i32)
        idx_now = sb("idx_now", [P, ORDER], i32)
        idx_first = sb("idx_first", [P, STEPS, ORDER], i32)
        eps_t = sb("eps_t", [P, TPS])
        mhalf = sb("mhalf", [P, TPS])
        w1h = sb("w1h", [P, DEPTH * DFF], f16)
        w1l = sb("w1l", [P, DEPTH * DFF], f16)
        w2 = sb("w2", [P, DEPTH, FC, DIM])
        woh = sb("woh", [P, VOCAB], f16)
        wol = sb("wol", [P, VOCAB], f16)
        weh = sb("weh", [P, VC, VOCAB], f16)
        wel = sb("wel", [P, VC, VOCAB], f16)
        bias_parts = sb("bias_parts", [P, VOCAB], bf16)
        cosT = sb("cosT", [P, DEPTH, SEQ])
        sinT = sb("sinT", [P, DEPTH, SEQ])
        b1p = sb("b1p", [P, DEPTH * FC])
        tokb_row = sb("tokb_row", [P, VOCAB])
        bo_row = sb("bo_row", [P, VOCAB])
        bin_row = sb("bin_row", [P, DIM])
        sm = sb("sm", [P, 96])
        G = sb("G", [P, STEPS, VOCAB])
        H1 = sb("H1", [P, STEPS, VOCAB])
        pacc = sb("pacc", [P, STEPS, DIM])
        h = [sb("hA", [P, TPS, DIM]), sb("hB", [P, TPS, DIM])]
        conv = sb("conv", [P, 7, SEQ])
        cz, cx, cxc, cxs, cur, cui, cy = (conv[:, n, :] for n in range(7))
        fz = sb("fz", [P, SEQ])
        fzh = sb("fzh", [P, SEQ], f16)
        fzl = sb("fzl", [P, SEQ], f16)
        fg = sb("fg", [P, FC, SEQ])
        fy = sb("fy", [P, SEQ])
        lzh = [sb("lzhA", [P, SEQ], f16), sb("lzhB", [P, SEQ], f16)]
        lzl = [sb("lzlA", [P, SEQ], f16), sb("lzlB", [P, SEQ], f16)]
        AR = sb("AR", [P, 4 * VOCAB])
        h2 = [AR[:, 0:VOCAB], AR[:, VOCAB:2 * VOCAB]]
        ez = AR[:, 2 * VOCAB:3 * VOCAB]
        ezh = AR[:, 3 * VOCAB:3 * VOCAB + HV].bitcast(f16)
        ezl = AR[:, 3 * VOCAB + HV:4 * VOCAB].bitcast(f16)
        ezT = sb("ezT", [P, 2, VOCAB], f16)
        st = {n: sb("st_" + n, [P, TPS, 12]) for n in "icfle"}
        mv = {n: sb("mv_" + n, [P, TPS, 2]) for n in "icfle"}
        ve = {n: sb("ve_" + n, [P, TPS]) for n in "icfle"}
        rs = {n: sb("rs_" + n, [P, TPS]) for n in "icfle"}

        TC = pb("TC", [P, SEQ])
        TF = pb("TF", [P, SEQ])
        F1 = [pb("F1a", [P, SEQ]), pb("F1b", [P, SEQ])]
        FO = pb("FO", [P, VOCAB])
        FT = [pb("FTh", [P, VOCAB], f16), pb("FTl", [P, VOCAB], f16)]

        wblk = [AR[:, 2048 * n:2048 * n + 2048].rearrange("p (v j) -> p v j", v=4) for n in range(2)]
        ptT = [fg[:, n, :] for n in range(2)]
        pt_rows = [fz[:, :].rearrange("p (t d) -> p t d", t=4), fy[:, :].rearrange("p (t d) -> p t d", t=4)]
        win_sb = conv[:, 0:2, :].rearrange("p a b -> p (a b)")
        winT = ezT[:, :, :].rearrange("p a b -> p (a b)").bitcast(f32).rearrange("p (v d) -> p v d", v=VC)
        w1f = H1[:, 0:2, :].rearrange("p a b -> p (a b)")
        wof = H1[:, 2, :]
        bfs = H1[:, 3, :]
        tmp = [H1[:, 4, :].rearrange("p (l m) -> p l m", l=DEPTH), H1[:, 5, :].rearrange("p (l m) -> p l m", l=DEPTH)]
        lnlb = H1[:, 6, 0:P]
        weff = H1
        la = conv[:, 0:4, :].rearrange("p a b -> p (a b)").rearrange("p (k i) -> p k i", k=KC)
        lb = fg[:, :, :].rearrange("p a b -> p (a b)").rearrange("p (k o) -> p k o", k=KC)

        def S(n, w=DEPTH):
            return sm[:, n:n + w]
        mag2, mag, rad, inv, cs1, sn1, t1, t2, t3, u0r, u0i = (S(4 * n) for n in range(11))
        cm, sm_ = S(44), S(48)
        wmax, wsc, wds = S(52, 3), S(56, 3), S(60, 3)
        bp4, lw = S(64, 1), S(66, 2)
        wmaxp = S(70, 3)
        stw, mvw = S(74, 12), S(86, 2)
        t4, = (S(88),)

        def pcol(name, n=0, w=1):
            return par[:, PCOLS[name][0] + n:PCOLS[name][0] + n + w]

        s_par, s_idx, s_rows, s_win, s_w1, s_wo, s_w2, s_weff, s_lora, s_bo = (
            sem(n) for n in ("par_in", "idx_in", "rows_in", "win_in", "w1_in", "wo_in", "w2_in",
                             "ffnw_in", "lora_in", "bout_in"))
        s_wblk = [sem("wblk_in0"), sem("wblk_in1")]
        s_const = sem("consts")
        s_id16 = sem("ident16_done")
        s_idx2 = sem("idx_offset")
        s_dv = sem("dve_setup")
        s_lo_chain = sem("vector_setup_chain")
        s_pl = sem("pool_setup")
        s_rad = sem("radius")
        s_pmag = sem("magnitude")
        s_winc, s_winp, s_winT, s_bpp, s_bp = (sem(n) for n in (
            "win_centred", "win_transposed", "win_t_copied", "bp_product", "bp_done"))
        s_ptp, s_pte, s_ptt, s_ptr = (sem(n) for n in (
            "ptab_product", "ptab_evacuated", "ptab_turned", "ptab_rows"))
        s_ptd = [sem("ptab_out0"), sem("ptab_out1")]
        s_ptl = sem("ptab_out_last")
        s_b1m, s_bom, s_lom = sem("b1_product"), sem("bo_product"), sem("lora_product")
        s_lad, s_max, s_red = sem("lora_added"), sem("wmax_part"), sem("wmax_all")
        s_hi, s_lo = sem("w_hi"), sem("w_lo")
        s_scaled = sem("w_scale")
        s_setup = sem("vector_ready")
        s_gi, s_gT, s_gP = sem("g_init"), sem("g_token_sum"), sem("g_projected_sum")
        s_ix, s_mv = sem("idx_now_ready"), sem("h1_moved")
        i_st, i_mv, i_ve, i_rs, i_h = (sem("in_" + n) for n in ("stats", "meanvar", "vareps", "rstd", "h"))
        c_st, c_mv, c_ve, c_rs, c_z, c_zT, c_x, c_rot, c_scan, c_prod, c_y, c_yT, c_h = (sem("conv_" + n) for n in (
            "stats", "meanvar", "vareps", "rstd", "z", "zT", "x", "rot", "scan", "prod", "y", "yT", "h"))
        f_st, f_mv, f_ve, f_rs, f_z, f_zT, f_zh, f_zl, f_f1, f_g, f_f2, f_y, f_yT, f_h = (sem("ffn_" + n) for n in (
            "stats", "meanvar", "vareps", "rstd", "z", "zT", "zh", "zl", "f1", "g", "f2", "y", "yT", "h"))
        l_st, l_mv, l_ve, l_rs, l_z, l_zT, l_zh, l_zl = (sem("last_" + n) for n in (
            "stats", "meanvar", "vareps", "rstd", "z", "zT", "zh", "zl"))
        e_wo, e_h2, e_st, e_mv, e_ve, e_rs, e_z, e_zh, e_zl, e_T, e_zT, e_mm, e_out = (sem("end_" + n) for n in (
            "wo", "h2", "stats", "meanvar", "vareps", "rstd", "z", "zh", "zl", "turned", "zT", "mm", "out"))
        s_out = [sem("out_dma0"), sem("out_dma1")]

        def after(eng, s, v):
            if not (isinstance(v, int) and v <= 0):
                eng.wait_ge(s, v)

        def held(eng, v):
            return v if isinstance(v, int) else eng.to_reg(v)

        class Round:
            def __init__(self, p):
                n = p if isinstance(p, int) else 3
                self.p = p
                self.layers = n < ROUNDS
                self.first, self.n = n == 0, n

            def ffn(self, k):
                return 0 <= STEPS * self.n + k - 1 < STEPS * ROUNDS

            def end(self, k):
                return self.n >= 1 and k < STEPS

            def end_mm(self, k):
                return 0 <= STEPS * (self.n - 1) + k - 1 < TILES

            def gather(self, k):
                return STEPS <= STEPS * self.n + 7 + k < TILES

        def rounds(eng, body):
            body(Round(0))
            body(Round(1))
            with eng.Fori(2, ROUNDS - 1) as p:
                body(Round(p))
            body(Round(ROUNDS - 1))
            body(Round(ROUNDS))

        block = ctx.enter_context(nc.Block())

        @block.sync
        def _(sp):
            sp.dma_start(par[:, :], cols).then_inc(s_par, 16)
            sp.dma_start(win_sb, win).then_inc(s_win, 16)
            sp.dma_start(idx_sb[:, :, :], idx).then_inc(s_idx, 16)
            sp.dma_start(tokb_row[:, :], tok_b.partition_broadcast(P)).then_inc(s_rows, 16)
            sp.dma_start(bin_row[:, :], bin_.partition_broadcast(P)).then_inc(s_rows, 16)
            tokv = tok_w.rearrange("(v p) j -> p v j", p=P)

            def block_in(j, n, half):
                sp.dma_start(wblk[half][:, :, 0:n], tokv[:, 4 * half:4 * half + 4, bass.ds(j, n)]).then_inc(s_wblk[half], 16)

            def rows_out(j, b, c):
                sp.wait_ge(s_ptr, c + 1)
                sp.dma_start(ptab[bass.ds(j, 512), :].rearrange("(t p) d -> p t d", p=P), pt_rows[b]).then_inc(s_ptd[b], 16)

            block_in(0, 512, 0)
            block_in(0, 512, 1)
            sp.dma_start(w1f, w1t).then_inc(s_w1, 16)
            sp.dma_start(wof, woutt).then_inc(s_wo, 16)
            sp.dma_start(bo_row[:, :], bout.partition_broadcast(P)).then_inc(s_bo, 16)
            sp.dma_start(bfs, ffn_bias.partition_broadcast(P)).then_inc(s_bo, 16)
            sp.dma_start(w2[:, :, :, :], w2t).then_inc(s_w2, 16)
            for b in range(8):
                n = 512 if b < 7 else ROWS - 8 * 512
                for half in range(2):
                    sp.wait_ge(s_ptp, 2 * b + half + 1)
                    block_in(512 * (b + 1), n, half)
                if b >= 1:
                    rows_out(512 * (b - 1), (b - 1) % 2, b - 1)
            rows_out(512 * 7, 1, 7)
            sp.wait_ge(s_ptr, 9)
            sp.dma_start(ptab[8 * 512:ROWS, :], pt_rows[0][0:ROWS - 8 * 512, 0, :]).then_inc(s_ptl, 16)
            sp.wait_ge(s_winp, 1)
            sp.dma_start(la, lora_a).then_inc(s_lora, 16)
            sp.wait_ge(s_ptt, 9)
            sp.dma_start(lb, lora_bt).then_inc(s_lora, 16)
            sp.wait_ge(s_setup, 1)
            sp.dma_start(weff[:, :, :], ffn_wt).then_inc(s_weff, 16)
            outv = out.rearrange("(t p) v -> t p v", p=P)

            def body(r):
                for k in range(STEPS + 1 if r.n == ROUNDS else STEPS):
                    if r.end_mm(k):
                        tau = STEPS * (r.p - 1) + k - 1
                        sp.wait_ge(e_out, 2 * tau + 2)
                        sp.dma_start(out[bass.ds(tau * P, P), :], h2[(k - 1) % 2]).then_inc(s_out[(k - 1) % 2], 16)
            rounds(sp, body)
            sp.wait_ge(s_out[0], 16 * TILES // 2)
            sp.wait_ge(s_out[1], 16 * TILES // 2)
            for b in range(2):
                sp.wait_ge(s_ptd[b], 64)
            sp.wait_ge(s_ptl, 16)

        @block.gpsimd
        def _(pool):
            nc.gpsimd.memset(ident[:, :], 0.0).then_inc(s_pl, 1)
            nc.gpsimd.memset(ones_b[:, :], 1.0)
            nc.gpsimd.memset(eps_t[:, :], EPS)
            nc.gpsimd.memset(mhalf[:, :], -0.5).then_inc(s_const, 1)
            pool.wait_ge(s_pl, 1)
            nc.gpsimd.affine_select(out=ident[:, :], in_=ident[:, :], compare_op=ALU.not_equal, fill=1.0, base=0,
                                    pattern=[[-1, P]], channel_multiplier=1).then_inc(s_const, 1)

            def gather_tok(slot, ix):
                nc.gpsimd.indirect_dma_start(G[:, slot, :], None, tok_wt, bass.IndirectOffsetOnAxis(ap=ix.bitcast(u32), axis=0),
                                             compute_op=ALU.add).then_inc(s_gT, 16)

            def gather_proj(slot, ix, first):
                nc.gpsimd.indirect_dma_start(pacc[:, slot, :], None, ptab, bass.IndirectOffsetOnAxis(ap=ix.bitcast(u32), axis=0),
                                             compute_op=ALU.bypass if first else ALU.add).then_inc(s_gP, 16)

            nc.gpsimd.memset(t4, 0.5).then_inc(s_pl, 1)
            pool.wait_ge(s_pl, 2)
            pool.wait_ge(s_dv, 1)
            nc.gpsimd.tensor_tensor(mag, mag2, t4, ALU.pow).then_inc(s_pmag, 1)
            pool.wait_ge(s_idx2, 4)
            nc.gpsimd.tensor_copy(idx_first[:, :, :], idx_sb[:, 0:STEPS, :]).then_inc(s_pl, 1)
            pool.wait_ge(s_pl, 3)
            pool.wait_ge(s_gi, STEPS)
            for k in range(ORDER):
                after(pool, s_gT, 16 * STEPS * k)
                for t in range(STEPS):
                    gather_tok(t, idx_first[:, t, k:k + 1])
            for b in range(2):
                pool.wait_ge(s_ptd[b], 64)
            pool.wait_ge(s_ptl, 16)
            for k in range(ORDER):
                after(pool, s_gP, 16 * STEPS * k)
                for t in range(STEPS):
                    gather_proj(t, idx_first[:, t, k:k + 1], k == 0)
                for n in {0: (0, 1), 3: (2,)}.get(k, ()):
                    pool.wait_ge(s_max, n + 1)
                    nc.gpsimd.partition_all_reduce(wmax[:, n:n + 1], wmaxp[:, n:n + 1], P, ABSMAX).then_inc(s_red, 1)

            def rstd(n, tiles, mvsem, vesem, rssem, v):
                pool.wait_ge(mvsem, v + 1)
                nc.gpsimd.tensor_tensor(ve[n][:, 0:tiles], mv[n][:, 0:tiles, 1], eps_t[:, 0:tiles], ALU.add).then_inc(vesem, 1)
                pool.wait_ge(vesem, v + 1)
                nc.gpsimd.tensor_tensor(rs[n][:, 0:tiles], ve[n][:, 0:tiles], mhalf[:, 0:tiles], ALU.pow).then_inc(rssem, 1)

            def body(r):
                p = r.p
                for k in range(STEPS):
                    def gather_round(kk):
                        if not r.gather(k):
                            return
                        tau, slot = STEPS * p + 7 + k, (7 + k) % STEPS
                        before = held(pool, 64 * tau + 16 * kk)
                        if kk > 0:
                            pool.wait_ge(s_const, 2)
                        pool.wait_ge(s_gT, before)
                        pool.wait_ge(s_gP, before)
                        if kk == 0:
                            nc.gpsimd.tensor_copy(idx_now[:, :], idx_sb[:, bass.ds(tau, 1), :].rearrange("p a b -> p (a b)")).then_inc(s_ix, 1)
                            turn, used = held(pool, tau + 1), held(pool, 2 * (p if k else p - 1) + slot // TPS + 1)
                            copied = held(pool, tau - STEPS + 1)
                            pool.wait_ge(s_const, 2)
                            pool.wait_ge(s_ix, copied)
                            pool.wait_ge(s_gi, turn)
                            pool.wait_ge(i_h, used)
                        gather_tok(slot, idx_now[:, kk:kk + 1])
                        gather_proj(slot, idx_now[:, kk:kk + 1], kk == 0)

                    if r.layers and k < 2:
                        rstd("i", TPS, i_mv, i_ve, i_rs, 2 * p + k)
                    if r.layers:
                        rstd("c", TPS, c_mv, c_ve, c_rs, STEPS * p + k)
                    if r.ffn(k):
                        rstd("f", TPS, f_mv, f_ve, f_rs, STEPS * p + k - 1)
                    gather_round(0)
                    if r.layers:
                        u, L = STEPS * p + k, k // 2
                        pool.wait_ge(c_x, u + 1)
                        after(pool, c_y, u)
                        nc.gpsimd.tensor_tensor(cxc, cx, cosT[:, L, :], ALU.mult).then_inc(c_rot, 1)
                        nc.gpsimd.tensor_tensor(cxs, cx, sinT[:, L, :], ALU.mult).then_inc(c_rot, 1)
                    gather_round(1)
                    if r.end(k):
                        rstd("e", 1, e_mv, e_ve, e_rs, STEPS * (p - 1) + k)
                    gather_round(2)
                    if r.layers and k == 7:
                        rstd("l", TPS, l_mv, l_ve, l_rs, 2 * p)
                    if r.n >= 1 and k == 0:
                        rstd("l", TPS, l_mv, l_ve, l_rs, 2 * p - 1)
                    gather_round(3)
            rounds(pool, body)

        @block.scalar
        def _(act):
            act.wait_ge(s_rows, 32)
            for t in range(STEPS):
                nc.scalar.activation(G[:, t, :], tokb_row[:, :], ACT.Copy).then_inc(s_gi, 1)
            act.wait_ge(s_winp, 1)
            nc.scalar.activation(winT.rearrange("p v d -> p (v d)"), FO[:, :], ACT.Copy).then_inc(s_winT, 1)
            act.wait_ge(s_pmag, 1)
            nc.scalar.activation(rad, mag, ACT.Tanh).then_inc(s_rad, 1)
            act.wait_ge(s_bp, 1)
            for b in range(9):
                n = 512 if b < 8 else ROWS - 8 * 512
                act.wait_ge(s_ptp, 2 * b + 2)
                if b >= 2:
                    act.wait_ge(s_ptt, b - 1)
                nc.scalar.activation(ptT[b % 2][:, 0:n], F1[b % 2][:, 0:n], ACT.Identity, bias=bp4).then_inc(s_pte, 1)
            act.wait_ge(s_scaled, 1)
            nc.scalar.activation(w1h[:, :], w1f, ACT.Identity, scale=wsc[:, 0:1]).then_inc(s_hi, 1)
            act.wait_ge(s_scaled, 2)
            nc.scalar.activation(woh[:, :], wof, ACT.Identity, scale=wsc[:, 1:2]).then_inc(s_hi, 1)
            act.wait_ge(s_scaled, 3)
            for v in range(VC):
                nc.scalar.activation(weh[:, v, :], weff[:, v, :], ACT.Identity, scale=wsc[:, 2:3]).then_inc(s_hi, 1)

            def body(r):
                p = r.p
                for k in range(STEPS):
                    u, uf, tau, L, Lf = STEPS * p + k, STEPS * p + k - 1, STEPS * (p - 1) + k, k // 2, (k - 1) % STEPS // 2
                    if r.gather(k):
                        slot = (7 + k) % STEPS
                        act.wait_ge(s_mv, STEPS * p + k)
                        nc.scalar.activation(G[:, slot, :], tokb_row[:, :], ACT.Copy).then_inc(s_gi, 1)
                    if r.layers:
                        act.wait_ge(c_zT, u + 1)
                        after(act, c_rot, 2 * u)
                        nc.scalar.activation(cx, TC[:, :], ACT.Silu, bias=pcol("ln1_b", L), scale=pcol("ln1_w", L)).then_inc(c_x, 1)
                    if r.ffn(k):
                        act.wait_ge(f_zT, uf + 1)
                        after(act, f_f1, 4 * uf)
                        nc.scalar.activation(fzh[:, :], TF[:, :], ACT.Copy, scale=ZUP).then_inc(f_zh, 1)
                        for c in range(FC):
                            act.wait_ge(f_f1, 4 * uf + c + 1)
                            after(act, f_f2, uf)
                            nc.scalar.activation(fg[:, c, :], F1[c % 2][:, :], ACT.Silu, bias=b1p[:, FC * Lf + c:FC * Lf + c + 1],
                                                 scale=wds[:, 0:1]).then_inc(f_g, 1)
                    if r.end(k):
                        act.wait_ge(e_z, tau + 1)
                        after(act, e_T, 2 * tau)
                        nc.scalar.activation(ezh, ez, ACT.Copy, scale=ZUP).then_inc(e_zh, 1)
                    if r.ffn(k):
                        act.wait_ge(f_f2, uf + 1)
                        after(act, f_yT, uf)
                        nc.scalar.activation(fy[:, :], TF[:, :], ACT.Identity, bias=pcol("b2", Lf)).then_inc(f_y, 1)
                    if r.end(k):
                        for n in range(2):
                            act.wait_ge(e_T, 2 * tau + n + 1)
                            after(act, e_mm, 2 * tau)
                            nc.scalar.activation(ezT[:, n, :], FT[n][:, :], ACT.Copy).then_inc(e_zT, 1)
                    if (r.layers and k == 7) or (r.n >= 1 and k == 0):
                        v, s = (2 * p, 0) if k == 7 else (2 * p - 1, 1)
                        act.wait_ge(l_zT, v + 1)
                        after(act, e_wo, STEPS * ((p if k == 7 else p - 1) - 1) + TPS * (s + 1))
                        nc.scalar.activation(lzh[s][:, :], TF[:, :], ACT.Copy, scale=ZUP).then_inc(l_zh, 1)
            rounds(act, body)

        @block.tensor
        def _(pe):
            mm = nc.tensor.matmul

            def turn(dst, src, n, idt=None):
                idt = ident if idt is None else idt
                for t in range(n):
                    last = nc.tensor.transpose(dst[:, P * t:P * t + P], src[:, P * t:P * t + P], idt[:, :])
                return last

            pe.wait_ge(s_const, 2)
            pe.wait_ge(s_winc, 1)
            turn(FO, win_sb, VC).then_inc(s_winp, 1)
            pe.wait_ge(s_winT, 1)
            pe.wait_ge(s_par, 16)
            for v in range(VC):
                last = mm(TC[:, 0:1], winT[:, v, :], pcol("tok_b", v), start=v == 0, stop=v == VC - 1)
            last.then_inc(s_bpp, 1)

            def turn_block(b):
                n = 4 if b < 8 else 1
                pe.wait_ge(s_pte, b + 1)
                if b >= 2:
                    pe.wait_ge(s_ptr, b - 1)
                dst = (TC, TF)[b % 2]
                if b < 8:
                    turn(dst, ptT[b % 2], 4).then_inc(s_ptt, 1)
                else:
                    w = ROWS - 8 * 512
                    nc.tensor.transpose(dst[0:w, 0:P], ptT[b % 2][:, 0:w], ident[:, :]).then_inc(s_ptt, 1)

            pe.wait_ge(s_bp, 1)
            for b in range(9):
                n = 512 if b < 8 else ROWS - 8 * 512
                if b >= 2:
                    pe.wait_ge(s_pte, b - 1)
                for half in range(2):
                    pe.wait_ge(s_wblk[half], 16 * (b + 1))
                    for v in range(4):
                        last = mm(F1[b % 2][:, 0:n], winT[:, 4 * half + v, :], wblk[half][:, v, 0:n],
                                  start=half == 0 and v == 0, stop=half == 1 and v == 3)
                    last.then_inc(s_ptp, 1)
                if b >= 1:
                    turn_block(b - 1)
            turn_block(8)
            pe.wait_ge(s_w1, 16)
            pe.wait_ge(s_pte, 9)
            for L in range(DEPTH):
                for c in range(FC):
                    n = FC * L + c
                    last = mm(F1[0][:, n:n + 1], w1f[:, P * n:P * n + P], pcol("ln2_b", L), start=True, stop=True)
            last.then_inc(s_b1m, 1)
            pe.wait_ge(s_wo, 16)
            pe.wait_ge(s_dv, 3)
            for n in range(2):
                last = mm(FO[:, n * HV:n * HV + HV], lnlb, wof[:, n * HV:n * HV + HV], start=True, stop=True)
            last.then_inc(s_bom, 1)
            pe.wait_ge(s_lad, 1)
            pe.wait_ge(s_lora, 32)
            for v in range(VC):
                for n in range(2):
                    c = 2 * v + n
                    if c >= 2:
                        pe.wait_ge(s_lad, c)
                    else:
                        pe.wait_ge(s_setup, 1)
                    for q in range(KC):
                        last = mm(F1[n][:, :], la[:, q, P * v:P * v + P], lb[:, q, n * HV:n * HV + HV],
                                  start=q == 0, stop=q == KC - 1)
                    last.then_inc(s_lom, 1)
            pe.wait_ge(s_w2, 16)
            pe.wait_ge(s_ptr, 9)
            pe.wait_ge(s_lo, 2)

            def split3(dst, wh, wl, ah, al, start, stop):
                mm(dst, wh, ah, start=start, stop=False)
                mm(dst, wl, ah, start=False, stop=False)
                return mm(dst, wh, al, start=False, stop=stop)

            def body(r):
                p = r.p
                for k in range(STEPS + 1 if r.n == ROUNDS else STEPS):
                    u, uf, tau, Lf = STEPS * p + k, STEPS * p + k - 1, STEPS * (p - 1) + k, (k - 1) % STEPS // 2
                    if r.end(k):
                        s, t = k // TPS, k % TPS
                        pe.wait_ge(l_zl, 2 * (p - 1) + s + 1)
                        after(pe, e_out, 2 * (tau - 1))
                        for n in range(2):
                            o = slice(n * HV, n * HV + HV)
                            mm(FO[:, o], lzh[s][:, P * t:P * t + P], woh[:, o], start=True, stop=False)
                            mm(FO[:, o], lzh[s][:, P * t:P * t + P], wol[:, o], start=False, stop=False)
                            last = mm(FO[:, o], lzl[s][:, P * t:P * t + P], woh[:, o], start=False, stop=True)
                        last.then_inc(e_wo, 1)
                    if r.layers and k < STEPS:
                        pe.wait_ge(c_z, u + 1)
                        after(pe, c_h, u)
                        turn(TC, cz, TPS).then_inc(c_zT, 1)
                    if r.ffn(k):
                        pe.wait_ge(f_z, uf + 1)
                        after(pe, f_h, uf)
                        if k == 0 or k == 1:
                            after(pe, l_zl, 2 * (p - 1) + k + 1)
                        turn(TF, fz, TPS).then_inc(f_zT, 1)

                    def end_half(n):
                        tp = tau - 1
                        pe.wait_ge(e_zT, 2 * tp + 2)
                        if r.end(k):
                            pe.wait_ge(e_h2, tau + 1)
                        else:
                            pe.wait_ge(e_out, 2 * tp)
                        o = slice(n * HV, n * HV + HV)
                        mm(FO[:, o], ones_b[:, :], bias_parts[:, o], start=True, stop=False)
                        for v in range(VC):
                            zh, zl = ezT[:, 0, P * v:P * v + P], ezT[:, 1, P * v:P * v + P]
                            mm(FO[:, o], zh, weh[:, v, o], start=False, stop=False)
                            mm(FO[:, o], zh, wel[:, v, o], start=False, stop=False)
                            last = mm(FO[:, o], zl, weh[:, v, o], start=False, stop=v == VC - 1)
                        last.then_inc(e_mm, 1)

                    if r.end_mm(k):
                        end_half(0)

                    def up(c):
                        after(pe, f_g, 4 * uf + c - 1)
                        w = slice(DFF * Lf + P * c, DFF * Lf + P * c + P)
                        split3(F1[c % 2][:, :], w1h[:, w], w1l[:, w], fzh[:, :], fzl[:, :], True, True).then_inc(f_f1, 1)

                    def down(c):
                        pe.wait_ge(f_g, 4 * uf + c + 1)
                        return mm(TF[:, :], w2[:, Lf, c, :], fg[:, c, :], start=c == 0, stop=c == FC - 1)

                    if r.ffn(k):
                        pe.wait_ge(f_zl, uf + 1)
                        up(0)
                        up(1)
                        up(2)
                        down(0)
                        up(3)
                        down(1)
                        down(2)
                        down(3).then_inc(f_f2, 1)
                    if r.layers and k < STEPS:
                        pe.wait_ge(c_y, u + 1)
                        turn(TC, cy, TPS).then_inc(c_yT, 1)
                    if r.end_mm(k):
                        end_half(1)
                    if r.ffn(k):
                        pe.wait_ge(f_y, uf + 1)
                        turn(TF, fy, TPS).then_inc(f_yT, 1)
                    if r.end(k):
                        after(pe, e_zT, 2 * tau)
                        pe.wait_ge(e_zh, tau + 1)
                        turn(FT[0], ezh, VC, ident16).then_inc(e_T, 1)
                        pe.wait_ge(e_zl, tau + 1)
                        turn(FT[1], ezl, VC, ident16).then_inc(e_T, 1)
                    if (r.layers and k == 7) or (r.n >= 1 and k == 0):
                        v = 2 * p if k == 7 else 2 * p - 1
                        pe.wait_ge(l_z, v + 1)
                        turn(TF, fz, TPS).then_inc(l_zT, 1)
            rounds(pe, body)

        @block.vector
        def _(dve):
            V = nc.vector
            done = [0]

            def chain(ins):
                done[0] += 1
                ins.then_inc(s_lo_chain, 1)
                dve.wait_ge(s_lo_chain, done[0])

            dve.wait_ge(s_par, 16)
            chain(V.tensor_tensor(t1, pcol("phz_re", 0, 4), pcol("phz_re", 0, 4), ALU.mult))
            chain(V.tensor_tensor(t2, pcol("phz_im", 0, 4), pcol("phz_im", 0, 4), ALU.mult))
            V.tensor_tensor(mag2, t1, t2, ALU.add).then_inc(s_dv, 1)
            dve.wait_ge(s_win, 16)
            chain(V.bn_stats(stw[:, 0:6], win_sb[:, 0:HV]))
            chain(V.bn_stats(stw[:, 6:12], win_sb[:, HV:VOCAB]))
            chain(V.bn_aggr(mvw, stw))
            V.tensor_scalar(win_sb, win_sb, mvw[:, 0:1], None, ALU.subtract).then_inc(s_winc, 1)
            dve.wait_ge(s_idx, 16)
            for k in range(ORDER):
                V.tensor_scalar(idx_sb[:, :, k], idx_sb[:, :, k], float(k * (VOCAB + 1)), None, ALU.add).then_inc(s_idx2, 1)
            dve.wait_ge(s_const, 2)
            V.tensor_copy(ident16[:, :], ident[:, :]).then_inc(s_id16, 1)
            dve.wait_ge(s_bpp, 1)
            V.tensor_scalar(bp4, TC[:, 0:1], 0.25, None, ALU.mult).then_inc(s_bp, 1)
            dve.wait_ge(s_pmag, 1)
            chain(V.tensor_scalar(inv, mag, 1e-30, None, ALU.max))
            chain(V.reciprocal(t3, inv))
            chain(V.tensor_scalar(inv, mag, 0.0, None, ALU.is_equal))
            chain(V.tensor_tensor(t1, pcol("phz_re", 0, 4), t3, ALU.mult))
            chain(V.tensor_tensor(cs1, t1, inv, ALU.add))
            chain(V.tensor_tensor(sn1, pcol("phz_im", 0, 4), t3, ALU.mult))
            chain(V.tensor_tensor(t1, cs1, cs1, ALU.mult))
            chain(V.tensor_tensor(t2, sn1, sn1, ALU.mult))
            chain(V.tensor_tensor(t3, t1, t2, ALU.add))
            chain(V.tensor_scalar(t3, t3, -0.5, 1.5, ALU.mult, ALU.add))
            chain(V.tensor_tensor(cm, cs1, t3, ALU.mult))
            chain(V.tensor_tensor(sm_, sn1, t3, ALU.mult))
            chain(V.tensor_tensor(t1, cm, pcol("lc_re", 0, 4), ALU.mult))
            chain(V.tensor_tensor(t2, sm_, pcol("lc_im", 0, 4), ALU.mult))
            chain(V.tensor_tensor(u0r, t1, t2, ALU.subtract))
            chain(V.tensor_tensor(t1, sm_, pcol("lc_re", 0, 4), ALU.mult))
            chain(V.tensor_tensor(t2, cm, pcol("lc_im", 0, 4), ALU.mult))
            chain(V.tensor_tensor(t3, t1, t2, ALU.add))
            chain(V.tensor_scalar(u0i, t3, -1.0, None, ALU.mult))
            chain(V.memset(cosT[:, :, 0:1], 1.0))
            chain(V.memset(sinT[:, :, 0:1], 0.0))
            pt = [0]

            def rows_copied():
                b = pt[0]
                if b > 8:
                    return
                pt[0] += 1
                dve.wait_ge(s_ptt, b + 1)
                if b >= 2:
                    dve.wait_ge(s_ptd[b % 2], 16 * (b // 2))
                w = ROWS - 8 * 512
                if b < 8:
                    V.tensor_copy(pt_rows[b % 2].rearrange("p t d -> p (t d)"), (TC, TF)[b % 2][:, :]).then_inc(s_ptr, 1)
                else:
                    V.tensor_copy(pt_rows[0][0:w, 0, :], TC[0:w, 0:P]).then_inc(s_ptr, 1)

            m = 1
            while m < SEQ:
                c4 = cm.rearrange("p (l o) -> p l o", o=1).to_broadcast([P, DEPTH, m])
                s4 = sm_.rearrange("p (l o) -> p l o", o=1).to_broadcast([P, DEPTH, m])
                C0, S0 = cosT[:, :, 0:m], sinT[:, :, 0:m]
                chain(V.tensor_tensor(tmp[0][:, :, 0:m], C0, c4, ALU.mult))
                chain(V.tensor_tensor(tmp[1][:, :, 0:m], S0, s4, ALU.mult))
                chain(V.tensor_tensor(cosT[:, :, m:2 * m], tmp[0][:, :, 0:m], tmp[1][:, :, 0:m], ALU.subtract))
                chain(V.tensor_tensor(tmp[0][:, :, 0:m], S0, c4, ALU.mult))
                chain(V.tensor_tensor(tmp[1][:, :, 0:m], C0, s4, ALU.mult))
                chain(V.tensor_tensor(sinT[:, :, m:2 * m], tmp[0][:, :, 0:m], tmp[1][:, :, 0:m], ALU.add))
                chain(V.tensor_tensor(t1, cm, cm, ALU.mult))
                chain(V.tensor_tensor(t2, sm_, sm_, ALU.mult))
                chain(V.tensor_tensor(t3, cm, sm_, ALU.mult))
                chain(V.tensor_tensor(cs1, t1, t2, ALU.subtract))
                chain(V.tensor_tensor(sn1, t1, t2, ALU.add))
                chain(V.tensor_scalar(sn1, sn1, -1.0, 2.0, ALU.mult, ALU.add))
                chain(V.tensor_tensor(cm, cs1, sn1, ALU.mult))
                chain(V.tensor_scalar(t3, t3, 2.0, None, ALU.mult))
                chain(V.tensor_tensor(sm_, t3, sn1, ALU.mult))
                m *= 2
                rows_copied()
            while pt[0] <= 8:
                rows_copied()
            dve.wait_ge(s_b1m, 1)
            chain(V.tensor_tensor(b1p[:, :], F1[0][:, 0:DEPTH * FC], pcol("b1", 0, DEPTH * FC), ALU.add))
            for L in range(DEPTH):
                chain(V.tensor_scalar(w1f[:, DFF * L:DFF * L + DFF], w1f[:, DFF * L:DFF * L + DFF], pcol("ln2_w", L), None, ALU.mult))
            V.tensor_reduce(wmaxp[:, 0:1], w1f, AX.X, ALU.max, apply_absolute_value=True).then_inc(s_max, 1)
            V.tensor_copy(lnlb, pcol("lnl_b").to_broadcast([P, P])).then_inc(s_dv, 2)
            dve.wait_ge(s_bom, 1)
            dve.wait_ge(s_bo, 32)
            chain(V.tensor_tensor(bo_row[:, :], bo_row[:, :], FO[:, :], ALU.add))
            chain(V.tensor_scalar(wof, wof, pcol("lnl_w"), None, ALU.mult))
            V.tensor_reduce(wmaxp[:, 1:2], wof, AX.X, ALU.max, apply_absolute_value=True).then_inc(s_max, 1)

            def scale(n):
                dve.wait_ge(s_red, n + 1)
                chain(V.tensor_scalar(wmax[:, n:n + 1], wmax[:, n:n + 1], 1e-30, None, ALU.max))
                chain(V.tensor_scalar(wds[:, n:n + 1], wmax[:, n:n + 1], 1.0 / (WUP * ZUP), None, ALU.mult))
                chain(V.reciprocal(wsc[:, n:n + 1], wmax[:, n:n + 1]))
                chain(V.tensor_scalar(wsc[:, n:n + 1], wsc[:, n:n + 1], WUP, None, ALU.mult))
                V.nop().then_inc(s_scaled, 1)

            scale(0)
            dve.wait_ge(s_hi, 1)
            chain(V.scalar_tensor_tensor(out=w1l[:, :], in0=w1f, scalar=wsc[:, 0:1], in1=w1h[:, :], op0=ALU.mult, op1=ALU.subtract))
            scale(1)
            dve.wait_ge(s_hi, 2)
            chain(V.scalar_tensor_tensor(out=wol[:, :], in0=wof, scalar=wsc[:, 1:2], in1=woh[:, :], op0=ALU.mult, op1=ALU.subtract))
            chain(V.tensor_tensor(lw, pcol("coeffs", 0, 2), pcol("scales", 0, 2), ALU.mult))
            dve.wait_ge(s_lora, 32)
            chain(V.tensor_scalar(lb[:, 0, :], lb[:, 0, :], lw[:, 0:1], None, ALU.mult))
            V.tensor_scalar(lb[:, 1, :], lb[:, 1, :], lw[:, 1:2], None, ALU.mult).then_inc(s_lad, 1)
            chain(V.tensor_copy(h2[0], bfs))
            V.nop().then_inc(s_setup, 1)
            dve.wait_ge(s_weff, 16)
            for v in range(VC):
                for n in range(2):
                    c = 2 * v + n
                    dve.wait_ge(s_lom, c + 1)
                    o = weff[:, v, n * HV:n * HV + HV]
                    V.tensor_tensor(o, o, F1[n][:, :], ALU.add).then_inc(s_lad, 1)
            dve.wait_ge(s_lad, 2 * VC + 1)
            V.tensor_reduce(wmaxp[:, 2:3], weff[:, :, :], AX.XY, ALU.max, apply_absolute_value=True).then_inc(s_max, 1)
            scale(2)
            for v in range(VC):
                dve.wait_ge(s_hi, 3 + v)
                chain(V.scalar_tensor_tensor(out=wel[:, v, :], in0=weff[:, v, :], scalar=wsc[:, 2:3], in1=weh[:, v, :],
                                             op0=ALU.mult, op1=ALU.subtract))
            chain(V.tensor_scalar(h2[0], h2[0], wsc[:, 2:3], ZUP, ALU.mult, ALU.mult))
            bh = ezh.bitcast(bf16)
            for q in range(3):
                chain(V.tensor_copy(bh, h2[0]))
                if q == 0:
                    chain(V.tensor_scalar(bias_parts[:, :], bh, ident[:, 0:1], None, ALU.mult))
                else:
                    chain(V.scalar_tensor_tensor(out=bias_parts[:, :], in0=bh, scalar=ident[:, q:q + 1], in1=bias_parts[:, :],
                                                 op0=ALU.mult, op1=ALU.add))
                if q < 2:
                    chain(V.tensor_tensor(h2[0], h2[0], bh, ALU.subtract))
            V.nop().then_inc(s_lo, 2)
            dve.wait_ge(s_rad, 1)
            dve.wait_ge(s_rows, 32)
            for b in range(2):
                dve.wait_ge(s_ptd[b], 64)
            dve.wait_ge(s_ptl, 16)

            def norm_stats(n, src, tiles, width, s_stat, s_mean, v):
                parts = max(1, width // 512)
                for t in range(tiles):
                    for q in range(parts):
                        w = width // parts
                        last = V.bn_stats(st[n][:, t, 6 * q:6 * q + 6], src(t)[:, q * w:q * w + w])
                last.then_inc(s_stat, 1)
                done_v = held(dve, v + 1)
                dve.wait_ge(s_const, 2)
                dve.wait_ge(s_stat, done_v)
                for t in range(tiles):
                    last = V.bn_aggr(mv[n][:, t, :], st[n][:, t, 0:6 * parts])
                last.then_inc(s_mean, 1)

            def normalise(n, dst, hs):
                for t in range(TPS):
                    last = V.tensor_scalar(dst[:, P * t:P * t + P], hs[:, t, :], mv[n][:, t, 0:1], rs[n][:, t:t + 1],
                                           ALU.subtract, ALU.mult)
                return last

            def body(r):
                p = r.p
                for k in range(STEPS + 1 if r.n == ROUNDS else STEPS):
                    u, uf, tau, L, Lf = STEPS * p + k, STEPS * p + k - 1, STEPS * (p - 1) + k, k // 2, (k - 1) % STEPS // 2
                    layers, ffn, end = r.layers, r.ffn(k), r.end(k)
                    hc, hf = h[k % 2], h[(k - 1) % 2]
                    flat = lambda a: a[:, :, :].rearrange("p t d -> p (t d)")
                    if layers and k < 2:
                        v = 2 * p + k
                        need = 64 * STEPS if r.first else 64 * (TPS * v + TPS)
                        dve.wait_ge(s_gT, need)
                        norm_stats("i", lambda t: G[:, TPS * k + t, :], TPS, VOCAB, i_st, i_mv, v)
                        dve.wait_ge(s_gP, need)
                        dve.wait_ge(i_rs, v + 1)
                        after(dve, l_z, v - 1)
                        for t in range(TPS):
                            last = V.scalar_tensor_tensor(out=hc[:, t, :], in0=pacc[:, TPS * k + t, :], scalar=rs["i"][:, t:t + 1],
                                                          in1=bin_row[:, :], op0=ALU.mult, op1=ALU.add)
                        last.then_inc(i_h, 1)
                    if layers:
                        if k < 2:
                            dve.wait_ge(i_h, 2 * p + k + 1)
                        else:
                            dve.wait_ge(f_h, u - 1)
                        norm_stats("c", lambda t: hc[:, t, :], TPS, DIM, c_st, c_mv, u)
                    if ffn:
                        dve.wait_ge(c_h, uf + 1)
                        norm_stats("f", lambda t: hf[:, t, :], TPS, DIM, f_st, f_mv, uf)
                    if layers:
                        dve.wait_ge(c_rs, u + 1)
                        after(dve, c_zT, u)
                        normalise("c", cz, hc).then_inc(c_z, 1)
                    if ffn:
                        dve.wait_ge(f_rs, uf + 1)
                        after(dve, f_zT, uf)
                        if k < 2:
                            after(dve, l_zT, 2 * (p - 1) + k + 1)
                        normalise("f", fz, hf).then_inc(f_z, 1)
                    if end:
                        dve.wait_ge(e_wo, tau + 1)
                        if not (r.n == 1 and k < 2):
                            dve.wait_ge(s_out[k % 2], 16 * ((STEPS // 2) * (p - 1) + k // 2))
                        dve.wait_ge(s_mv, tau + 1)
                        V.scalar_tensor_tensor(out=h2[k % 2], in0=FO[:, :], scalar=wds[:, 1:2], in1=H1[:, k, :],
                                               op0=ALU.mult, op1=ALU.add).then_inc(e_h2, 1)
                        dve.wait_ge(e_h2, tau + 1)
                        norm_stats("e", lambda t: h2[k % 2], 1, VOCAB, e_st, e_mv, tau)
                    if layers:
                        V.tensor_tensor(H1[:, k, :], G[:, k, :], bo_row[:, :], ALU.add).then_inc(s_mv, 1)
                    if ffn:
                        dve.wait_ge(f_zh, uf + 1)
                        after(dve, f_f1, 4 * uf)
                        V.scalar_tensor_tensor(out=fzl[:, :], in0=TF[:, :], scalar=ZUP, in1=fzh[:, :],
                                               op0=ALU.mult, op1=ALU.subtract).then_inc(f_zl, 1)
                    if end:
                        dve.wait_ge(e_rs, tau + 1)
                        after(dve, e_zl, tau)
                        V.tensor_scalar(ez, h2[k % 2], mv["e"][:, 0, 0:1], rs["e"][:, 0:1], ALU.subtract, ALU.mult).then_inc(e_z, 1)
                    if layers:
                        rb = rad[:, L:L + 1].to_broadcast([P, SEQ])
                        for n, (src, dst, u0) in enumerate(((cxc, cur, u0r), (cxs, cui, u0i))):
                            dve.wait_ge(c_rot, 2 * u + n + 1)
                            V.tensor_tensor_scan(dst, rb, src, u0[:, L:L + 1], ALU.mult, ALU.add).then_inc(c_scan, 1)
                        for n, (src, dst, tab) in enumerate(((cur, cxc, cosT), (cui, cxs, sinT))):
                            dve.wait_ge(c_scan, 2 * u + n + 1)
                            V.scalar_tensor_tensor(out=dst, in0=src, scalar=pcol("sc_lin", L), in1=tab[:, L, :],
                                                   op0=ALU.mult, op1=ALU.mult).then_inc(c_prod, 1)
                        dve.wait_ge(c_prod, 2 * u + 2)
                        after(dve, c_yT, u)
                        V.tensor_tensor(cy, cxc, cxs, ALU.add).then_inc(c_y, 1)
                    if end:
                        dve.wait_ge(e_zh, tau + 1)
                        after(dve, e_T, 2 * tau)
                        V.scalar_tensor_tensor(out=ezl, in0=ez, scalar=ZUP, in1=ezh, op0=ALU.mult, op1=ALU.subtract).then_inc(e_zl, 1)

                    def end_sum(n):
                        tp = tau - 1
                        dve.wait_ge(e_mm, 2 * tp + n + 1)
                        o = slice(n * HV, n * HV + HV)
                        hb = h2[(k - 1) % 2][:, o]
                        V.scalar_tensor_tensor(out=hb, in0=FO[:, o], scalar=wds[:, 2:3], in1=hb, op0=ALU.mult, op1=ALU.add).then_inc(e_out, 1)

                    if r.end_mm(k):
                        end_sum(0)
                    if layers:
                        dve.wait_ge(c_yT, u + 1)
                        V.tensor_tensor(flat(hc), flat(hc), TC[:, :], ALU.add).then_inc(c_h, 1)
                    if ffn:
                        dve.wait_ge(f_yT, uf + 1)
                        V.tensor_tensor(flat(hf), flat(hf), TF[:, :], ALU.add).then_inc(f_h, 1)
                    if (layers and k == 7) or (r.n >= 1 and k == 0):
                        v, s = (2 * p, 0) if k == 7 else (2 * p - 1, 1)
                        dve.wait_ge(f_h, uf + 1)
                        norm_stats("l", lambda t: h[s][:, t, :], TPS, DIM, l_st, l_mv, v)
                        dve.wait_ge(l_rs, v + 1)
                        normalise("l", fz, h[s]).then_inc(l_z, 1)
                        dve.wait_ge(l_zh, v + 1)
                        V.scalar_tensor_tensor(out=lzl[s][:, :], in0=TF[:, :], scalar=ZUP, in1=lzh[s][:, :],
                                               op0=ALU.mult, op1=ALU.subtract).then_inc(l_zl, 1)
                    if r.end_mm(k):
                        end_sum(1)
            rounds(dve, body)


def kernel(x, L0_tok_W, L0_tok_b, L0_attn_Win, L0_attn_bin, L0_attn_ln1_w, L0_attn_ln1_b, L0_attn_phz_re,
           L0_attn_phz_im, L0_attn_lc_re, L0_attn_lc_im, L0_attn_sc_lin, L0_attn_ln2_w, L0_attn_ln2_b, L0_attn_W1,
           L0_attn_b1, L0_attn_W2, L0_attn_b2, L0_attn_lnl_w, L0_attn_lnl_b, L0_attn_Wout, L0_attn_bout, L0_ffn_W,
           L0_ffn_bias, L0_ffn_A, L0_ffn_Bf, L0_ffn_coeffs, L0_ffn_scales):
    import numpy as np
    import concourse.bacc as bacc
    from concourse.bass_utils import run_bass_kernel_spmd

    a = lambda v: np.asarray(v)
    c = np.ascontiguousarray
    xs = a(x)
    ctxs = np.stack([np.pad(xs, ((0, 0), (s, 0)), constant_values=VOCAB)[:, :SEQ] for s in (3, 2, 1, 0)], -1)
    idx = c(ctxs.reshape(TILES, P, ORDER).transpose(1, 0, 2))
    per_ch = lambda v, n: a(v).reshape(n, P).T
    parts = {
        "ln1_w": per_ch(L0_attn_ln1_w, 4), "ln1_b": per_ch(L0_attn_ln1_b, 4), "phz_re": per_ch(L0_attn_phz_re, 4),
        "phz_im": per_ch(L0_attn_phz_im, 4), "lc_re": per_ch(L0_attn_lc_re, 4), "lc_im": per_ch(L0_attn_lc_im, 4),
        "sc_lin": per_ch(L0_attn_sc_lin, 4), "ln2_w": per_ch(L0_attn_ln2_w, 4), "ln2_b": per_ch(L0_attn_ln2_b, 4),
        "b2": per_ch(L0_attn_b2, 4), "b1": per_ch(L0_attn_b1, 16), "lnl_w": per_ch(L0_attn_lnl_w, 1),
        "lnl_b": per_ch(L0_attn_lnl_b, 1), "tok_b": per_ch(L0_tok_b, 8),
        "coeffs": np.repeat(a(L0_ffn_coeffs), 16).reshape(2, P).T, "scales": np.repeat(a(L0_ffn_scales), 16).reshape(2, P).T,
    }
    cols = c(np.concatenate([parts[n] for n in PCOLS], 1))
    chunks = lambda m: c(m.reshape(-1, P, m.shape[-1]).transpose(1, 0, 2))
    W1 = a(L0_attn_W1)
    arrays = {
        "idx": idx, "tok_wt": c(a(L0_tok_W).T), "tok_w": c(a(L0_tok_W)), "cols": cols, "tok_b": c(a(L0_tok_b)),
        "win": c(a(L0_attn_Win)), "bin": c(a(L0_attn_bin)),
        "w1t": c(W1.transpose(2, 0, 1).reshape(P, DEPTH * DFF)),
        "w2t": c(a(L0_attn_W2).transpose(0, 2, 1).reshape(DEPTH, DFF // P, P, DIM).transpose(2, 0, 1, 3)),
        "woutt": c(a(L0_attn_Wout).T), "bout": c(a(L0_attn_bout)), "ffn_wt": chunks(a(L0_ffn_W).T), "ffn_bias": c(a(L0_ffn_bias)),
        "lora_a": chunks(a(L0_ffn_A).reshape(EXP, VOCAB)),
        "lora_bt": chunks(c(a(L0_ffn_Bf).transpose(0, 2, 1)).reshape(EXP, VOCAB)),
    }
    nc = bacc.Bacc("TRN2", target_bir_lowering=False, num_devices=1)
    args = [nc.dram_tensor(n, v.shape, mybir.dt.from_np(v.dtype), kind="ExternalInput").ap() for n, v in arrays.items()]
    out = nc.dram_tensor("out", (NSEQ * SEQ, VOCAB), mybir.dt.float32, kind="ExternalOutput").ap()
    ptab = nc.dram_tensor("ptab", (ROWS, DIM), mybir.dt.float32, kind="Internal").ap()
    program(nc, *args, out, ptab)
    r = run_bass_kernel_spmd(nc, [arrays], core_ids=[0])
    return r.results[0]["out"].reshape(NSEQ, SEQ, VOCAB)
```

```python
import concourse.bass as bass
from concourse import mybir
from contextlib import ExitStack

P = 128
ABSMAX = bass.bass_isa.ReduceOp.absmax
VOCAB, DIM, DFF, DEPTH = 1024, 128, 512, 4
NSEQ, SEQ = 16, 512
ORDER = 4
EXP = 16 * 16
TILES = NSEQ * SEQ // P
TPS = SEQ // P
STEPS = 2 * TPS
ROUNDS = NSEQ // 2
ROWS = ORDER * (VOCAB + 1)
EPS = 1e-5
ZUP = 256.0
WUP = 4096.0
PCOLS = {}
_at = 0
for _n, _w in (("ln1_w", 4), ("ln1_b", 4), ("phz_re", 4), ("phz_im", 4), ("lc_re", 4), ("lc_im", 4),
               ("sc_lin", 4), ("ln2_w", 4), ("ln2_b", 4), ("b2", 4), ("b1", 16), ("lnl_w", 1),
               ("lnl_b", 1), ("tok_b", 8), ("coeffs", 2), ("scales", 2)):
    PCOLS[_n] = (_at, _w)
    _at += _w
PWIDTH = _at


def program(nc, idx, tok_wt, tok_w, cols, tok_b, win, bin_, w1t, w2t, woutt, bout, ffn_wt, ffn_bias,
            lora_a, lora_bt, out, ptab, tok3):
    f32, f16, bf16, i32 = mybir.dt.float32, mybir.dt.float16, mybir.dt.bfloat16, mybir.dt.int32
    u32 = mybir.dt.uint32
    ALU, ACT, AX = mybir.AluOpType, mybir.ActivationFunctionType, mybir.AxisListType
    HV = VOCAB // 2
    VC = VOCAB // P
    FC = DFF // P
    KC = EXP // P

    ctx = ExitStack()
    with ctx:
        def sb(name, shape, dt=f32):
            return ctx.enter_context(nc.sbuf_tensor(name, shape, dt))

        def pb(name, shape, dt=f32):
            return ctx.enter_context(nc.psum_tensor(name, shape, dt))

        def sem(name):
            return ctx.enter_context(nc.semaphore(name))

        ident = sb("ident", [P, P])
        ident16 = sb("ident16", [P, P], f16)
        ones_b = sb("ones_b", [P, P], bf16)
        par = sb("par", [P, PWIDTH])
        idx_sb = sb("idx_sb", [P, TILES, ORDER + 1], i32)
        idx_now = sb("idx_now", [P, ORDER + 1], i32)
        idx_first = sb("idx_first", [P, STEPS, ORDER + 1], i32)
        eps_t = sb("eps_t", [P, TPS])
        mhalf = sb("mhalf", [P, TPS])
        w1h = sb("w1h", [P, DEPTH * DFF], f16)
        w1l = sb("w1l", [P, DEPTH * DFF], f16)
        w2 = sb("w2", [P, DEPTH, FC, DIM])
        woh = sb("woh", [P, VOCAB], f16)
        wol = sb("wol", [P, VOCAB], f16)
        weh = sb("weh", [P, VC, VOCAB], f16)
        wel = sb("wel", [P, VC, VOCAB], f16)
        bias_parts = sb("bias_parts", [P, VOCAB], bf16)
        cosT = sb("cosT", [P, DEPTH, SEQ])
        sinT = sb("sinT", [P, DEPTH, SEQ])
        b1p = sb("b1p", [P, DEPTH * FC])
        bo_row = sb("bo_row", [P, VOCAB])
        bin_row = sb("bin_row", [P, DIM])
        sm = sb("sm", [P, 96])
        G = sb("G", [P, STEPS, VOCAB])
        H1 = sb("H1", [P, STEPS, VOCAB])
        pacc = sb("pacc", [P, STEPS, DIM])
        h = [sb("hA", [P, TPS, DIM]), sb("hB", [P, TPS, DIM])]
        conv = sb("conv", [P, 6, SEQ])
        cz, cx, cxc, cxs, cur, cui = (conv[:, n, :] for n in range(6))
        cy = cx
        fz = sb("fz", [P, SEQ])
        fzh = sb("fzh", [P, SEQ], f16)
        fzl = sb("fzl", [P, SEQ], f16)
        fg = sb("fg", [P, FC, SEQ])
        fy = sb("fy", [P, SEQ])
        lzf = sb("lzf", [P, P])
        lzh = [sb("lzhA", [P, SEQ], f16), sb("lzhB", [P, SEQ], f16)]
        lzl = [sb("lzlA", [P, SEQ], f16), sb("lzlB", [P, SEQ], f16)]
        AR = sb("AR", [P, 4 * VOCAB])
        h2 = [AR[:, 0:VOCAB], AR[:, VOCAB:2 * VOCAB]]
        ez = AR[:, 2 * VOCAB:3 * VOCAB]
        ezh = AR[:, 3 * VOCAB:3 * VOCAB + HV].bitcast(f16)
        ezl = AR[:, 3 * VOCAB + HV:4 * VOCAB].bitcast(f16)
        ezT = [sb("ezT0", [P, 2, VOCAB], f16), sb("ezT1", [P, 2, VOCAB], f16)]
        oh = sb("oh", [P, HV])
        st = {n: sb("st_" + n, [P, TPS, 12]) for n in "cfle"}
        mv = {n: sb("mv_" + n, [P, TPS, 2]) for n in "cfle"}
        ve = {n: sb("ve_" + n, [P, TPS]) for n in "cfle"}
        rs = {n: sb("rs_" + n, [P, TPS]) for n in "cfle"}
        st["i"], mv["i"] = sb("st_i", [P, STEPS, 12]), sb("mv_i", [P, STEPS, 2])
        ve["i"], rs["i"] = sb("ve_i", [P, STEPS]), sb("rs_i", [P, STEPS])

        TC = pb("TC", [P, SEQ])
        TF = pb("TF", [P, SEQ])
        F1 = [pb("F1a", [P, SEQ]), pb("F1b", [P, SEQ])]
        FO = pb("FO", [P, VOCAB])
        FW = pb("FW", [P, VOCAB])
        FT = [FW[:, n * HV:n * HV + HV].bitcast(f16) for n in range(2)]

        wblk = [AR[:, 2048 * n:2048 * n + 2048].rearrange("p (v j) -> p v j", v=4) for n in range(2)]
        ptT = [fg[:, n, :] for n in range(2)]
        pt_rows = [fz[:, :].rearrange("p (t d) -> p t d", t=4), fy[:, :].rearrange("p (t d) -> p t d", t=4)]
        win_sb = conv[:, 4:6, :].rearrange("p a b -> p (a b)")
        tokb_row = w2[:, 0:2, :, :].rearrange("p a b c -> p (a b c)")
        tok3s = [w[:, :, :].rearrange("p a b -> p (a b)").bitcast(f32).rearrange("p (t v) -> p t v", t=4) for w in (weh, wel)]
        winT = ezT[0][:, :, :].rearrange("p a b -> p (a b)").bitcast(f32).rearrange("p (v d) -> p v d", v=VC)
        w1f = G[:, 4:6, :].rearrange("p a b -> p (a b)")
        wof, bfs = G[:, 6, :], G[:, 7, :]
        bh = G[:, 4, 0:HV].bitcast(bf16)
        la = conv[:, 0:4, :].rearrange("p a b -> p (a b)").rearrange("p (k i) -> p k i", k=KC)
        lb = fg[:, :, :].rearrange("p a b -> p (a b)").rearrange("p (k o) -> p k o", k=KC)
        tmp = [conv[:, 2 * n:2 * n + 2, :].rearrange("p a b -> p (a b)").rearrange("p (l m) -> p l m", l=DEPTH) for n in range(2)]
        lnlb = lzf[:, :]
        weff = H1

        def S(n, w=DEPTH):
            return sm[:, n:n + w]
        mag2, mag, rad, inv, cs1, sn1, t1, t2, t3, u0r, u0i = (S(4 * n) for n in range(11))
        cm, sm_ = S(44), S(48)
        wmax, wsc, wds = S(52, 3), S(56, 3), S(60, 3)
        bp4, lw = S(64, 1), S(66, 2)
        wmaxp = S(70, 3)
        stw, mvw = S(74, 12), S(86, 2)
        t4, = (S(88),)

        def pcol(name, n=0, w=1):
            return par[:, PCOLS[name][0] + n:PCOLS[name][0] + n + w]

        s_par, s_idx, s_rows, s_win, s_w1, s_wo, s_w2, s_weff, s_lora, s_bo = (
            sem(n) for n in ("par_in", "idx_in", "rows_in", "win_in", "w1_in", "wo_in", "w2_in",
                             "ffnw_in", "lora_in", "bout_in"))
        s_wblk = [sem("wblk_in0"), sem("wblk_in1")]
        s_const = sem("consts")
        s_id16 = sem("ident16_done")
        s_idx2 = sem("idx_offset")
        s_dv = sem("dve_setup")
        s_lo_chain = sem("vector_setup_chain")
        s_pl = sem("pool_setup")
        s_rad = sem("radius")
        s_pmag = sem("magnitude")
        s_winc, s_winp, s_winT, s_bpp, s_bp = (sem(n) for n in (
            "win_centred", "win_transposed", "win_t_copied", "bp_product", "bp_done"))
        s_ptp, s_pte, s_ptt, s_ptr = (sem(n) for n in (
            "ptab_product", "ptab_evacuated", "ptab_turned", "ptab_rows"))
        s_ptd = [sem("ptab_out0"), sem("ptab_out1")]
        s_ptl = sem("ptab_out_last")
        s_b1m, s_bom, s_lom = sem("b1_product"), sem("bo_product"), sem("lora_product")
        s_lad, s_max, s_red = sem("lora_added"), sem("wmax_part"), sem("wmax_all")
        s_hi, s_lo = sem("w_hi"), sem("w_lo")
        s_scaled = sem("w_scale")
        s_setup = sem("vector_ready")
        s_t3i, s_t3a, s_t3o = sem("tok3_in"), sem("tok3_added"), sem("tok3_out")
        s_gT, s_gP = sem("g_token_sum"), sem("g_projected_sum")
        s_ix, s_mv = sem("idx_now_ready"), sem("h1_moved")
        i_st, i_mv, i_ve, i_rs, i_h = (sem("in_" + n) for n in ("stats", "meanvar", "vareps", "rstd", "h"))
        c_st, c_mv, c_ve, c_rs, c_z, c_zT, c_x, c_rot, c_scan, c_prod, c_y, c_yT, c_h = (sem("conv_" + n) for n in (
            "stats", "meanvar", "vareps", "rstd", "z", "zT", "x", "rot", "scan", "prod", "y", "yT", "h"))
        f_st, f_mv, f_ve, f_rs, f_z, f_zT, f_zh, f_zl, f_f1, f_g, f_f2, f_y, f_yT, f_h = (sem("ffn_" + n) for n in (
            "stats", "meanvar", "vareps", "rstd", "z", "zT", "zh", "zl", "f1", "g", "f2", "y", "yT", "h"))
        l_st, l_mv, l_ve, l_rs, l_z, l_zT, l_zh, l_zl = (sem("last_" + n) for n in (
            "stats", "meanvar", "vareps", "rstd", "z", "zT", "zh", "zl"))
        e_wo, e_h2, e_st, e_mv, e_ve, e_rs, e_z, e_zh, e_zl, e_T, e_zT, e_mm, e_out = (sem("end_" + n) for n in (
            "wo", "h2", "stats", "meanvar", "vareps", "rstd", "z", "zh", "zl", "turned", "zT", "mm", "out"))
        s_out = [sem("out_dma0"), sem("out_dma1")]
        s_out_b = sem("out_dma_second_half")

        def after(eng, s, v):
            if not (isinstance(v, int) and v <= 0):
                eng.wait_ge(s, v)

        def held(eng, v):
            return v if isinstance(v, int) else eng.to_reg(v)

        class Round:
            def __init__(self, p):
                n = p if isinstance(p, int) else 3
                self.p = p
                self.layers = n < ROUNDS
                self.first, self.n = n == 0, n

            def ffn(self, k):
                return 0 <= STEPS * self.n + k - 1 < STEPS * ROUNDS

            def end(self, k):
                return self.n >= 1 and k < STEPS

            def end_mm(self, k):
                return 0 <= STEPS * (self.n - 1) + k - 1 < TILES

            def end_late(self, k):
                return 0 <= STEPS * (self.n - 1) + k - 2 < TILES

            def gather(self, k):
                return STEPS <= STEPS * self.n + 7 + k < TILES

            def stats(self, k):
                return STEPS <= STEPS * self.n + 6 + k < TILES

            def last(self, k):
                return k == 7 and self.layers or k == 0 and self.n >= 1

            def steps(self):
                return STEPS + 2 if self.n == ROUNDS else STEPS

        def rounds(eng, body):
            body(Round(0))
            body(Round(1))
            with eng.Fori(2, ROUNDS - 1) as p:
                body(Round(p))
            body(Round(ROUNDS - 1))
            body(Round(ROUNDS))

        block = ctx.enter_context(nc.Block())

        @block.sync
        def _(sp):
            sp.dma_start(par[:, :], cols).then_inc(s_par, 16)
            sp.dma_start(win_sb, win).then_inc(s_win, 16)
            sp.dma_start(la, lora_a).then_inc(s_lora, 16)
            sp.dma_start(lb, lora_bt).then_inc(s_lora, 16)
            sp.dma_start(idx_sb[:, :, :], idx).then_inc(s_idx, 16)
            sp.dma_start(tokb_row[:, :], tok_b.partition_broadcast(P)).then_inc(s_rows, 16)
            sp.dma_start(bin_row[:, :], bin_.partition_broadcast(P)).then_inc(s_rows, 16)
            sp.dma_start(weff[:, :, :], ffn_wt).then_inc(s_weff, 16)
            t3 = tok_wt[(ORDER - 1) * (VOCAB + 1):(ORDER - 1) * (VOCAB + 1) + VOCAB, :].rearrange("(g t p) v -> g p t v", p=P, t=4)
            for n in range(2):
                sp.dma_start(tok3s[n], t3[n]).then_inc(s_t3i, 16)
            sp.dma_start(w1f, w1t).then_inc(s_w1, 16)
            sp.dma_start(wof, woutt).then_inc(s_wo, 16)
            sp.dma_start(bo_row[:, :], bout.partition_broadcast(P)).then_inc(s_bo, 16)
            sp.dma_start(bfs, ffn_bias.partition_broadcast(P)).then_inc(s_bo, 16)
            tokv = tok_w.rearrange("(v p) j -> p v j", p=P)

            def block_in(j, n, half):
                sp.dma_start(wblk[half][:, :, 0:n], tokv[:, 4 * half:4 * half + 4, bass.ds(j, n)]).then_inc(s_wblk[half], 16)

            def rows_out(b):
                sp.wait_ge(s_ptr, b + 1)
                sp.dma_start(ptab[bass.ds(512 * b, 512), :].rearrange("(t p) d -> p t d", p=P), pt_rows[b % 2]).then_inc(s_ptd[b % 2], 16)

            block_in(0, 512, 0)
            block_in(0, 512, 1)
            for b in range(8):
                n = 512 if b < 7 else ROWS - 8 * 512
                for half in range(2):
                    sp.wait_ge(s_ptp, 2 * b + half + 1)
                    block_in(512 * (b + 1), n, half)
                if b == 0:
                    for n in range(2):
                        sp.wait_ge(s_t3a, n + 1)
                        sp.dma_start(tok3.rearrange("(g t p) v -> g p t v", p=P, t=4)[n], tok3s[n]).then_inc(s_t3o, 16)
                    sp.dma_start(w2[:, :, :, :], w2t).then_inc(s_w2, 16)
                if b >= 1:
                    rows_out(b - 1)
            rows_out(7)
            sp.wait_ge(s_ptr, 9)
            sp.dma_start(ptab[8 * 512:ROWS, :], pt_rows[0][0:ROWS - 8 * 512, 0, :]).then_inc(s_ptl, 16)

            def body(r):
                for k in range(r.steps()):
                    if r.end_late(k):
                        tau = STEPS * (r.p - 1) + k - 2
                        sp.wait_ge(e_out, 2 * tau + 2)
                        sp.dma_start(out[bass.ds(tau * P, P), HV:VOCAB], oh[:, :]).then_inc(s_out_b, 16)
                    if r.end_mm(k):
                        tau = STEPS * (r.p - 1) + k - 1
                        sp.wait_ge(e_out, 2 * tau + 1)
                        sp.dma_start(out[bass.ds(tau * P, P), 0:HV], h2[(k - 1) % 2][:, 0:HV]).then_inc(s_out[(k - 1) % 2], 16)
            rounds(sp, body)
            sp.wait_ge(s_out[0], 16 * TILES // 2)
            sp.wait_ge(s_out[1], 16 * TILES // 2)
            sp.wait_ge(s_out_b, 16 * TILES)
            for b in range(2):
                sp.wait_ge(s_ptd[b], 64)
            sp.wait_ge(s_ptl, 16)
            sp.wait_ge(s_t3o, 32)

        @block.gpsimd
        def _(pool):
            nc.gpsimd.memset(ident[:, :], 0.0).then_inc(s_pl, 1)
            nc.gpsimd.memset(ones_b[:, :], 1.0)
            nc.gpsimd.memset(eps_t[:, :], EPS)
            nc.gpsimd.memset(mhalf[:, :], -0.5).then_inc(s_const, 1)
            pool.wait_ge(s_pl, 1)
            nc.gpsimd.affine_select(out=ident[:, :], in_=ident[:, :], compare_op=ALU.not_equal, fill=1.0, base=0,
                                    pattern=[[-1, P]], channel_multiplier=1).then_inc(s_const, 1)

            def gather_tok(slot, ix, k):
                q = k if k < ORDER - 1 else ORDER
                nc.gpsimd.indirect_dma_start(G[:, slot, :], None, tok3 if k == ORDER - 1 else tok_wt,
                                             bass.IndirectOffsetOnAxis(ap=ix[:, q:q + 1].bitcast(u32), axis=0),
                                             compute_op=ALU.bypass if k == 0 else ALU.add).then_inc(s_gT, 16)

            def gather_proj(slot, ix, first, rows=ROWS):
                nc.gpsimd.indirect_dma_start(pacc[:, slot, :], None, ptab[0:rows, :], bass.IndirectOffsetOnAxis(ap=ix.bitcast(u32), axis=0),
                                             compute_op=ALU.bypass if first else ALU.add).then_inc(s_gP, 16)

            nc.gpsimd.memset(t4, 0.5).then_inc(s_pl, 1)
            pool.wait_ge(s_pl, 2)
            pool.wait_ge(s_dv, 1)
            nc.gpsimd.tensor_tensor(mag, mag2, t4, ALU.pow).then_inc(s_pmag, 1)
            pool.wait_ge(s_idx2, 4)
            nc.gpsimd.tensor_copy(idx_first[:, :, :], idx_sb[:, 0:STEPS, :]).then_inc(s_pl, 1)
            pool.wait_ge(s_pl, 3)

            def first_tokens(s):
                for k in range(ORDER):
                    if k == ORDER - 1:
                        pool.wait_ge(s_t3o, 32)
                    after(pool, s_gT, 16 * TPS * (ORDER * s + k))
                    for t in range(TPS * s, TPS * s + TPS):
                        gather_tok(t, idx_first[:, t, :], k)

            first_tokens(0)
            for n in range(3):
                pool.wait_ge(s_max, n + 1)
                nc.gpsimd.partition_all_reduce(wmax[:, n:n + 1], wmaxp[:, n:n + 1], P, ABSMAX).then_inc(s_red, 1)
            for k in range(ORDER):
                last = ((k + 1) * (VOCAB + 1) - 1) // 512
                if k == 1:
                    pool.wait_ge(s_setup, 1)
                    first_tokens(1)
                pool.wait_ge(s_ptd[0], 16 * min(last // 2 + 1, 4))
                pool.wait_ge(s_ptd[1], 16 * min((last + 1) // 2, 4))
                if last == 8:
                    pool.wait_ge(s_ptl, 16)
                after(pool, s_gP, 16 * STEPS * k)
                for t in range(STEPS):
                    if k == ORDER - 1 and t == TPS:
                        pool.wait_ge(s_gP, 16 * (STEPS * k + TPS))
                    gather_proj(t, idx_first[:, t, k:k + 1], k == 0, (k + 1) * (VOCAB + 1))

            def rstd(n, tiles, mvsem, vesem, rssem, v, at=0):
                q = slice(at, at + tiles)
                pool.wait_ge(mvsem, v + 1)
                nc.gpsimd.tensor_tensor(ve[n][:, q], mv[n][:, q, 1], eps_t[:, 0:tiles], ALU.add).then_inc(vesem, 1)
                pool.wait_ge(vesem, v + 1)
                nc.gpsimd.tensor_tensor(rs[n][:, q], ve[n][:, q], mhalf[:, 0:tiles], ALU.pow).then_inc(rssem, 1)

            for t in range(TPS):
                rstd("i", 1, i_mv, i_ve, i_rs, t, t)

            def body(r):
                p = r.p
                for k in range(STEPS):
                    def gather_round(kk):
                        if not r.gather(k):
                            return
                        tau, slot = STEPS * p + 7 + k, (7 + k) % STEPS
                        before = held(pool, 64 * tau + 16 * kk)
                        if kk > 0:
                            pool.wait_ge(s_const, 2)
                        pool.wait_ge(s_gT, before)
                        pool.wait_ge(s_gP, before)
                        if kk == 0:
                            nc.gpsimd.tensor_copy(idx_now[:, :], idx_sb[:, bass.ds(tau, 1), :].rearrange("p a b -> p (a b)")).then_inc(s_ix, 1)
                            moved, used = held(pool, tau - STEPS + 1), held(pool, 2 * (p if k else p - 1) + slot // TPS + 1)
                            copied = held(pool, tau - STEPS + 1)
                            pool.wait_ge(s_const, 2)
                            pool.wait_ge(s_ix, copied)
                            pool.wait_ge(s_mv, moved)
                            pool.wait_ge(i_h, used)
                        gather_tok(slot, idx_now[:, :], kk)
                        gather_proj(slot, idx_now[:, kk:kk + 1], kk == 0)

                    if r.first and k == 1:
                        for t in range(TPS, STEPS):
                            rstd("i", 1, i_mv, i_ve, i_rs, t, t)
                    if r.stats(k) and k < 2:
                        rstd("i", 1, i_mv, i_ve, i_rs, STEPS * p + 6 + k, (6 + k) % STEPS)
                    if r.layers:
                        rstd("c", TPS, c_mv, c_ve, c_rs, STEPS * p + k)
                    if r.ffn(k):
                        rstd("f", TPS, f_mv, f_ve, f_rs, STEPS * p + k - 1)
                    gather_round(0)
                    if r.layers:
                        u, L = STEPS * p + k, k // 2
                        pool.wait_ge(c_x, u + 1)
                        after(pool, c_y, u)
                        nc.gpsimd.tensor_tensor(cxc, cx, cosT[:, L, :], ALU.mult).then_inc(c_rot, 1)
                        nc.gpsimd.tensor_tensor(cxs, cx, sinT[:, L, :], ALU.mult).then_inc(c_rot, 1)
                    gather_round(1)
                    if r.end(k):
                        rstd("e", 1, e_mv, e_ve, e_rs, STEPS * (p - 1) + k)
                    gather_round(2)
                    gather_round(3)
                    if r.stats(k) and k >= 2:
                        rstd("i", 1, i_mv, i_ve, i_rs, STEPS * p + 6 + k, (6 + k) % STEPS)
                    if r.last(k):
                        rstd("l", TPS, l_mv, l_ve, l_rs, 2 * p - (k == 0))
            rounds(pool, body)

        @block.scalar
        def _(act):
            act.wait_ge(s_winp, 1)
            nc.scalar.activation(winT.rearrange("p v d -> p (v d)"), FO[:, :], ACT.Copy).then_inc(s_winT, 1)
            act.wait_ge(s_pmag, 1)
            nc.scalar.activation(rad, mag, ACT.Tanh).then_inc(s_rad, 1)
            def high(dst, src, n):
                nc.scalar.activation(dst, src, ACT.Identity, scale=wsc[:, n:n + 1]).then_inc(s_hi, 1)

            def rows_copied(b):
                act.wait_ge(s_ptt, b + 1)
                if b >= 2:
                    act.wait_ge(s_ptd[b % 2], 16 * (b // 2))
                w = ROWS - 8 * 512
                if b < 8:
                    nc.scalar.activation(pt_rows[b % 2].rearrange("p t d -> p (t d)"), (TC, TF)[b % 2][:, :], ACT.Copy).then_inc(s_ptr, 1)
                else:
                    nc.scalar.activation(pt_rows[0][0:w, 0, :], TC[0:w, 0:P], ACT.Copy).then_inc(s_ptr, 1)

            act.wait_ge(s_bp, 1)
            for b in range(9):
                n = 512 if b < 8 else ROWS - 8 * 512
                act.wait_ge(s_ptp, 2 * b + 2)
                if b >= 2:
                    act.wait_ge(s_ptt, b - 1)
                nc.scalar.activation(ptT[b % 2][:, 0:n], F1[b % 2][:, 0:n], ACT.Identity, bias=bp4).then_inc(s_pte, 1)
                if b >= 1:
                    rows_copied(b - 1)
                if b == 2:
                    act.wait_ge(s_scaled, 1)
                    for v in range(VC):
                        high(weh[:, v, :], weff[:, v, :], 0)
                if b == 3:
                    act.wait_ge(s_scaled, 2)
                    high(w1h[:, :], w1f, 1)
                    act.wait_ge(s_scaled, 3)
                    high(woh[:, :], wof, 2)
            rows_copied(8)
            def body(r):
                p = r.p
                for k in range(STEPS):
                    u, uf, tau, L, Lf = STEPS * p + k, STEPS * p + k - 1, STEPS * (p - 1) + k, k // 2, (k - 1) % STEPS // 2
                    if r.layers:
                        act.wait_ge(c_zT, u + 1)
                        after(act, c_yT, u)
                        nc.scalar.activation(cx, TC[:, :], ACT.Silu, bias=pcol("ln1_b", L), scale=pcol("ln1_w", L)).then_inc(c_x, 1)
                    if r.ffn(k):
                        act.wait_ge(f_zT, uf + 1)
                        after(act, f_f1, 4 * uf)
                        nc.scalar.activation(fzh[:, :], TF[:, :], ACT.Copy, scale=ZUP).then_inc(f_zh, 1)
                        for c in range(FC):
                            act.wait_ge(f_f1, 4 * uf + c + 1)
                            after(act, f_f2, uf)
                            nc.scalar.activation(fg[:, c, :], F1[c % 2][:, :], ACT.Silu, bias=b1p[:, FC * Lf + c:FC * Lf + c + 1],
                                                 scale=wds[:, 1:2]).then_inc(f_g, 1)
                    if r.end(k):
                        act.wait_ge(e_z, tau + 1)
                        after(act, e_T, 2 * tau)
                        nc.scalar.activation(ezh, ez, ACT.Copy, scale=ZUP).then_inc(e_zh, 1)
                    if r.ffn(k):
                        act.wait_ge(f_f2, uf + 1)
                        after(act, f_yT, uf)
                        if k < 2:
                            after(act, l_zT, 2 * (p - 1) + k + 1)
                        nc.scalar.activation(fy[:, :], TF[:, :], ACT.Identity, bias=pcol("b2", Lf)).then_inc(f_y, 1)
                    if r.end(k):
                        for n in range(2):
                            act.wait_ge(e_T, 2 * tau + n + 1)
                            after(act, e_mm, 2 * tau - 2)
                            nc.scalar.activation(ezT[k % 2][:, n, :], FT[n], ACT.Copy).then_inc(e_zT, 1)
                    if r.last(k):
                        v, s = (2 * p, 0) if k == 7 else (2 * p - 1, 1)
                        act.wait_ge(l_zT, v + 1)
                        after(act, e_wo, STEPS * ((p if k == 7 else p - 1) - 1) + TPS * (s + 1))
                        nc.scalar.activation(lzh[s][:, :], F1[0][:, :], ACT.Copy, scale=ZUP).then_inc(l_zh, 1)
            rounds(act, body)

        @block.tensor
        def _(pe):
            mm = nc.tensor.matmul

            def turn(dst, src, n, idt=None):
                idt = ident if idt is None else idt
                for t in range(n):
                    last = nc.tensor.transpose(dst[:, P * t:P * t + P], src[:, P * t:P * t + P], idt[:, :])
                return last

            pe.wait_ge(s_const, 2)
            pe.wait_ge(s_winc, 1)
            turn(FO, win_sb, VC).then_inc(s_winp, 1)
            pe.wait_ge(s_winT, 1)
            pe.wait_ge(s_par, 16)
            for v in range(VC):
                last = mm(TC[:, 0:1], winT[:, v, :], pcol("tok_b", v), start=v == 0, stop=v == VC - 1)
            last.then_inc(s_bpp, 1)

            pe.wait_ge(s_bp, 1)
            pe.wait_ge(s_lad, 1)
            pe.wait_ge(s_lora, 32)
            for v in range(VC):
                for n in range(2):
                    c = 2 * v + n
                    if c >= 2:
                        pe.wait_ge(s_lad, c)
                    for q in range(KC):
                        last = mm(F1[n][:, :], la[:, q, P * v:P * v + P], lb[:, q, n * HV:n * HV + HV],
                                  start=q == 0, stop=q == KC - 1)
                    last.then_inc(s_lom, 1)
            pe.wait_ge(s_w1, 16)
            for L in range(DEPTH):
                for c in range(FC):
                    n = FC * L + c
                    last = mm(FO[:, n:n + 1], w1f[:, P * n:P * n + P], pcol("ln2_b", L), start=True, stop=True)
            last.then_inc(s_b1m, 1)
            pe.wait_ge(s_wo, 16)
            pe.wait_ge(s_dv, 3)
            for n in range(2):
                last = mm(FW[:, n * HV:n * HV + HV], lnlb, wof[:, n * HV:n * HV + HV], start=True, stop=True)
            last.then_inc(s_bom, 1)

            def turn_block(b):
                pe.wait_ge(s_pte, b + 1)
                if b >= 2:
                    pe.wait_ge(s_ptr, b - 1)
                dst = (TC, TF)[b % 2]
                if b < 8:
                    turn(dst, ptT[b % 2], 4).then_inc(s_ptt, 1)
                else:
                    w = ROWS - 8 * 512
                    nc.tensor.transpose(dst[0:w, 0:P], ptT[b % 2][:, 0:w], ident[:, :]).then_inc(s_ptt, 1)

            pe.wait_ge(s_lad, 2 * VC + 1)
            for b in range(9):
                n = 512 if b < 8 else ROWS - 8 * 512
                if b >= 2:
                    pe.wait_ge(s_pte, b - 1)
                for half in range(2):
                    pe.wait_ge(s_wblk[half], 16 * (b + 1))
                    for v in range(4):
                        last = mm(F1[b % 2][:, 0:n], winT[:, 4 * half + v, :], wblk[half][:, v, 0:n],
                                  start=half == 0 and v == 0, stop=half == 1 and v == 3)
                    last.then_inc(s_ptp, 1)
                if b >= 1:
                    turn_block(b - 1)
            turn_block(8)
            pe.wait_ge(s_w2, 16)
            pe.wait_ge(s_ptr, 9)
            pe.wait_ge(s_lo, 2)

            def split3(dst, wh, wl, ah, al, start, stop):
                mm(dst, wh, ah, start=start, stop=False)
                mm(dst, wl, ah, start=False, stop=False)
                return mm(dst, wh, al, start=False, stop=stop)

            def body(r):
                p = r.p
                for k in range(STEPS + 1 if r.n == ROUNDS else STEPS):
                    u, uf, tau, Lf = STEPS * p + k, STEPS * p + k - 1, STEPS * (p - 1) + k, (k - 1) % STEPS // 2
                    def project():
                        s, t = k // TPS, k % TPS
                        pe.wait_ge(l_zl, 2 * (p - 1) + s + 1)
                        after(pe, e_zT, 2 * tau)
                        for n in range(2):
                            o = slice(n * HV, n * HV + HV)
                            mm(FW[:, o], lzh[s][:, P * t:P * t + P], woh[:, o], start=True, stop=False)
                            mm(FW[:, o], lzh[s][:, P * t:P * t + P], wol[:, o], start=False, stop=False)
                            last = mm(FW[:, o], lzl[s][:, P * t:P * t + P], woh[:, o], start=False, stop=True)
                        last.then_inc(e_wo, 1)

                    if r.end(k) and k > 0:
                        project()
                    if r.layers:
                        pe.wait_ge(c_z, u + 1)
                        after(pe, c_h, u)
                        turn(TC, cz, TPS).then_inc(c_zT, 1)
                    if r.ffn(k):
                        pe.wait_ge(f_z, uf + 1)
                        after(pe, f_h, uf)
                        turn(TF, fz, TPS).then_inc(f_zT, 1)
                    if r.end(k) and k == 0:
                        project()

                    def end_half(n):
                        tp = tau - 1
                        pe.wait_ge(e_zT, 2 * tp + 2)
                        after(pe, e_out, 2 * tp - 1 + n)
                        o = slice(n * HV, n * HV + HV)
                        mm(FO[:, o], ones_b[:, :], bias_parts[:, o], start=True, stop=False)
                        for v in range(VC):
                            zT = ezT[(k - 1) % 2]
                            zh, zl = zT[:, 0, P * v:P * v + P], zT[:, 1, P * v:P * v + P]
                            mm(FO[:, o], zh, weh[:, v, o], start=False, stop=False)
                            mm(FO[:, o], zh, wel[:, v, o], start=False, stop=False)
                            last = mm(FO[:, o], zl, weh[:, v, o], start=False, stop=v == VC - 1)
                        last.then_inc(e_mm, 1)

                    if r.end_mm(k):
                        end_half(0)

                    def up(c):
                        after(pe, f_g, 4 * uf + c - 1)
                        if k < 2 and c == 0:
                            after(pe, l_zl, 2 * (p - 1) + k + 1)
                        w = slice(DFF * Lf + P * c, DFF * Lf + P * c + P)
                        split3(F1[c % 2][:, :], w1h[:, w], w1l[:, w], fzh[:, :], fzl[:, :], True, True).then_inc(f_f1, 1)

                    def down(c):
                        pe.wait_ge(f_g, 4 * uf + c + 1)
                        return mm(TF[:, :], w2[:, Lf, c, :], fg[:, c, :], start=c == 0, stop=c == FC - 1)

                    if r.ffn(k):
                        pe.wait_ge(f_zl, uf + 1)
                        up(0)
                        up(1)
                        up(2)
                        down(0)
                        up(3)
                        down(1)
                        down(2)
                        down(3).then_inc(f_f2, 1)
                    if r.layers:
                        pe.wait_ge(c_y, u + 1)
                        turn(TC, cy, TPS).then_inc(c_yT, 1)
                    if r.end(k):
                        pe.wait_ge(e_zh, tau + 1)
                        turn(FT[0], ezh, VC, ident16).then_inc(e_T, 1)
                        pe.wait_ge(e_zl, tau + 1)
                        turn(FT[1], ezl, VC, ident16).then_inc(e_T, 1)
                    if r.ffn(k):
                        pe.wait_ge(f_y, uf + 1)
                        turn(TF, fy, TPS).then_inc(f_yT, 1)
                    if r.end_mm(k):
                        end_half(1)
                    if r.last(k):
                        pe.wait_ge(l_z, 2 * p - (k == 0) + 1)
                        turn(F1[0], fy, TPS).then_inc(l_zT, 1)
            rounds(pe, body)

        @block.vector
        def _(dve):
            V = nc.vector
            done = [0]

            def chain(ins):
                done[0] += 1
                ins.then_inc(s_lo_chain, 1)
                dve.wait_ge(s_lo_chain, done[0])

            dve.wait_ge(s_par, 16)
            chain(V.tensor_tensor(t1, pcol("phz_re", 0, 4), pcol("phz_re", 0, 4), ALU.mult))
            chain(V.tensor_tensor(t2, pcol("phz_im", 0, 4), pcol("phz_im", 0, 4), ALU.mult))
            V.tensor_tensor(mag2, t1, t2, ALU.add).then_inc(s_dv, 1)
            dve.wait_ge(s_win, 16)
            chain(V.bn_stats(stw[:, 0:6], win_sb[:, 0:HV]))
            chain(V.bn_stats(stw[:, 6:12], win_sb[:, HV:VOCAB]))
            chain(V.bn_aggr(mvw, stw))
            V.tensor_scalar(win_sb, win_sb, mvw[:, 0:1], None, ALU.subtract).then_inc(s_winc, 1)
            chain(V.tensor_tensor(lw, pcol("coeffs", 0, 2), pcol("scales", 0, 2), ALU.mult))
            dve.wait_ge(s_lora, 32)
            chain(V.tensor_scalar(lb[:, 0, :], lb[:, 0, :], lw[:, 0:1], None, ALU.mult))
            V.tensor_scalar(lb[:, 1, :], lb[:, 1, :], lw[:, 1:2], None, ALU.mult).then_inc(s_lad, 1)
            dve.wait_ge(s_idx, 16)
            for k in range(ORDER):
                V.tensor_scalar(idx_sb[:, :, k], idx_sb[:, :, k], float(k * (VOCAB + 1)), None, ALU.add).then_inc(s_idx2, 1)
            dve.wait_ge(s_const, 2)
            V.tensor_copy(ident16[:, :], ident[:, :]).then_inc(s_id16, 1)
            V.tensor_copy(lnlb, pcol("lnl_b").to_broadcast([P, P])).then_inc(s_dv, 2)
            dve.wait_ge(s_bpp, 1)
            V.tensor_scalar(bp4, TC[:, 0:1], 0.25, None, ALU.mult).then_inc(s_bp, 1)
            dve.wait_ge(s_rows, 32)
            for n in range(2):
                dve.wait_ge(s_t3i, 32)
                bb = tokb_row.rearrange("p (o v) -> p o v", o=1).to_broadcast([P, 4, VOCAB])
                V.tensor_tensor(tok3s[n], tok3s[n], bb, ALU.add).then_inc(s_t3a, 1)
            dve.wait_ge(s_weff, 16)
            for v in range(VC):
                for n in range(2):
                    c = 2 * v + n
                    dve.wait_ge(s_lom, c + 1)
                    o = weff[:, v, n * HV:n * HV + HV]
                    V.tensor_tensor(o, o, F1[n][:, :], ALU.add).then_inc(s_lad, 1)
            dve.wait_ge(s_lad, 2 * VC + 1)
            V.tensor_reduce(wmaxp[:, 0:1], weff[:, :, :], AX.XY, ALU.max, apply_absolute_value=True).then_inc(s_max, 1)
            dve.wait_ge(s_b1m, 1)
            chain(V.tensor_tensor(b1p[:, :], FO[:, 0:DEPTH * FC], pcol("b1", 0, DEPTH * FC), ALU.add))
            for L in range(DEPTH):
                chain(V.tensor_scalar(w1f[:, DFF * L:DFF * L + DFF], w1f[:, DFF * L:DFF * L + DFF], pcol("ln2_w", L), None, ALU.mult))
            V.tensor_reduce(wmaxp[:, 1:2], w1f, AX.X, ALU.max, apply_absolute_value=True).then_inc(s_max, 1)
            dve.wait_ge(s_bom, 1)
            dve.wait_ge(s_bo, 32)
            chain(V.tensor_tensor(bo_row[:, :], bo_row[:, :], FW[:, :], ALU.add))
            chain(V.tensor_scalar(wof, wof, pcol("lnl_w"), None, ALU.mult))
            V.tensor_reduce(wmaxp[:, 2:3], wof, AX.X, ALU.max, apply_absolute_value=True).then_inc(s_max, 1)

            def scale(n):
                dve.wait_ge(s_red, n + 1)
                chain(V.tensor_scalar(wmax[:, n:n + 1], wmax[:, n:n + 1], 1e-30, None, ALU.max))
                chain(V.tensor_scalar(wds[:, n:n + 1], wmax[:, n:n + 1], 1.0 / (WUP * ZUP), None, ALU.mult))
                chain(V.reciprocal(wsc[:, n:n + 1], wmax[:, n:n + 1]))
                chain(V.tensor_scalar(wsc[:, n:n + 1], wsc[:, n:n + 1], WUP, None, ALU.mult))
                V.nop().then_inc(s_scaled, 1)

            for n in range(3):
                scale(n)
            for v in range(VC):
                dve.wait_ge(s_hi, 1 + v)
                chain(V.scalar_tensor_tensor(out=wel[:, v, :], in0=weff[:, v, :], scalar=wsc[:, 0:1], in1=weh[:, v, :],
                                             op0=ALU.mult, op1=ALU.subtract))
            dve.wait_ge(s_hi, VC + 1)
            chain(V.scalar_tensor_tensor(out=w1l[:, :], in0=w1f, scalar=wsc[:, 1:2], in1=w1h[:, :], op0=ALU.mult, op1=ALU.subtract))
            dve.wait_ge(s_hi, VC + 2)
            chain(V.scalar_tensor_tensor(out=wol[:, :], in0=wof, scalar=wsc[:, 2:3], in1=woh[:, :], op0=ALU.mult, op1=ALU.subtract))
            chain(V.tensor_scalar(bfs, bfs, wsc[:, 0:1], ZUP, ALU.mult, ALU.mult))
            for q in range(3):
                chain(V.tensor_copy(bh, bfs))
                if q == 0:
                    chain(V.tensor_scalar(bias_parts[:, :], bh, ident[:, 0:1], None, ALU.mult))
                else:
                    chain(V.scalar_tensor_tensor(out=bias_parts[:, :], in0=bh, scalar=ident[:, q:q + 1], in1=bias_parts[:, :],
                                                 op0=ALU.mult, op1=ALU.add))
                if q < 2:
                    chain(V.tensor_tensor(bfs, bfs, bh, ALU.subtract))
            V.nop().then_inc(s_setup, 1)
            dve.wait_ge(s_pmag, 1)
            chain(V.tensor_scalar(inv, mag, 1e-30, None, ALU.max))
            chain(V.reciprocal(t3, inv))
            chain(V.tensor_scalar(inv, mag, 0.0, None, ALU.is_equal))
            chain(V.tensor_tensor(t1, pcol("phz_re", 0, 4), t3, ALU.mult))
            chain(V.tensor_tensor(cs1, t1, inv, ALU.add))
            chain(V.tensor_tensor(sn1, pcol("phz_im", 0, 4), t3, ALU.mult))
            chain(V.tensor_tensor(t1, cs1, cs1, ALU.mult))
            chain(V.tensor_tensor(t2, sn1, sn1, ALU.mult))
            chain(V.tensor_tensor(t3, t1, t2, ALU.add))
            chain(V.tensor_scalar(t3, t3, -0.5, 1.5, ALU.mult, ALU.add))
            chain(V.tensor_tensor(cm, cs1, t3, ALU.mult))
            chain(V.tensor_tensor(sm_, sn1, t3, ALU.mult))
            chain(V.tensor_tensor(t1, cm, pcol("lc_re", 0, 4), ALU.mult))
            chain(V.tensor_tensor(t2, sm_, pcol("lc_im", 0, 4), ALU.mult))
            chain(V.tensor_tensor(u0r, t1, t2, ALU.subtract))
            chain(V.tensor_tensor(t1, sm_, pcol("lc_re", 0, 4), ALU.mult))
            chain(V.tensor_tensor(t2, cm, pcol("lc_im", 0, 4), ALU.mult))
            chain(V.tensor_tensor(t3, t1, t2, ALU.add))
            chain(V.tensor_scalar(u0i, t3, -1.0, None, ALU.mult))
            chain(V.memset(cosT[:, :, 0:1], 1.0))
            chain(V.memset(sinT[:, :, 0:1], 0.0))
            m = 1
            while m < SEQ:
                c4 = cm.rearrange("p (l o) -> p l o", o=1).to_broadcast([P, DEPTH, m])
                s4 = sm_.rearrange("p (l o) -> p l o", o=1).to_broadcast([P, DEPTH, m])
                C0, S0 = cosT[:, :, 0:m], sinT[:, :, 0:m]
                chain(V.tensor_tensor(tmp[0][:, :, 0:m], C0, c4, ALU.mult))
                chain(V.tensor_tensor(tmp[1][:, :, 0:m], S0, s4, ALU.mult))
                chain(V.tensor_tensor(cosT[:, :, m:2 * m], tmp[0][:, :, 0:m], tmp[1][:, :, 0:m], ALU.subtract))
                chain(V.tensor_tensor(tmp[0][:, :, 0:m], S0, c4, ALU.mult))
                chain(V.tensor_tensor(tmp[1][:, :, 0:m], C0, s4, ALU.mult))
                chain(V.tensor_tensor(sinT[:, :, m:2 * m], tmp[0][:, :, 0:m], tmp[1][:, :, 0:m], ALU.add))
                chain(V.tensor_tensor(t1, cm, cm, ALU.mult))
                chain(V.tensor_tensor(t2, sm_, sm_, ALU.mult))
                chain(V.tensor_tensor(t3, cm, sm_, ALU.mult))
                chain(V.tensor_tensor(cs1, t1, t2, ALU.subtract))
                chain(V.tensor_tensor(sn1, t1, t2, ALU.add))
                chain(V.tensor_scalar(sn1, sn1, -1.0, 2.0, ALU.mult, ALU.add))
                chain(V.tensor_tensor(cm, cs1, sn1, ALU.mult))
                chain(V.tensor_scalar(t3, t3, 2.0, None, ALU.mult))
                chain(V.tensor_tensor(sm_, t3, sn1, ALU.mult))
                m *= 2
            V.nop().then_inc(s_lo, 2)
            dve.wait_ge(s_rad, 1)
            dve.wait_ge(s_rows, 32)

            def norm_stats(n, src, tiles, width, s_stat, s_mean, v):
                parts = max(1, width // 512)
                for t in range(tiles):
                    for q in range(parts):
                        w = width // parts
                        last = V.bn_stats(st[n][:, t, 6 * q:6 * q + 6], src(t)[:, q * w:q * w + w])
                last.then_inc(s_stat, 1)
                done_v = held(dve, v + 1)
                dve.wait_ge(s_const, 2)
                dve.wait_ge(s_stat, done_v)
                for t in range(tiles):
                    last = V.bn_aggr(mv[n][:, t, :], st[n][:, t, 0:6 * parts])
                last.then_inc(s_mean, 1)

            def normalise(n, dst, hs):
                for t in range(TPS):
                    last = V.tensor_scalar(dst[:, P * t:P * t + P], hs[:, t, :], mv[n][:, t, 0:1], rs[n][:, t:t + 1],
                                           ALU.subtract, ALU.mult)
                return last

            def tile_stats(slot, tau):
                whole = STEPS * ORDER * 16
                dve.wait_ge(s_gT, whole // 2 if isinstance(tau, int) and tau < TPS else
                            whole if isinstance(tau, int) and tau < STEPS else 64 * tau + 64)
                for q in range(2):
                    last = V.bn_stats(st["i"][:, slot, 6 * q:6 * q + 6], G[:, slot, q * HV:q * HV + HV])
                last.then_inc(i_st, 1)
                done_v = held(dve, tau + 1)
                dve.wait_ge(s_const, 2)
                dve.wait_ge(i_st, done_v)
                V.bn_aggr(mv["i"][:, slot, :], st["i"][:, slot, :]).then_inc(i_mv, 1)

            for t in range(TPS):
                tile_stats(t, t)
            for b in range(2):
                dve.wait_ge(s_ptd[b], 64)
            dve.wait_ge(s_ptl, 16)

            def body(r):
                p = r.p
                for k in range(r.steps()):
                    u, uf, tau, L, Lf = STEPS * p + k, STEPS * p + k - 1, STEPS * (p - 1) + k, k // 2, (k - 1) % STEPS // 2
                    layers, ffn, end = r.layers, r.ffn(k), r.end(k)
                    hc, hf = h[k % 2], h[(k - 1) % 2]
                    flat = lambda a: a[:, :, :].rearrange("p t d -> p (t d)")
                    if r.first and k == 1:
                        for t in range(TPS, STEPS):
                            tile_stats(t, t)
                    if r.stats(k) and k < 2:
                        tile_stats((6 + k) % STEPS, STEPS * p + 6 + k)
                    if layers and k < 2:
                        v = 2 * p + k
                        dve.wait_ge(s_gP, (16 * 28 if k == 0 else 512) if r.first else 64 * (TPS * v + TPS))
                        dve.wait_ge(i_rs, TPS * v + TPS)
                        after(dve, l_z, v - 1)
                        for t in range(TPS):
                            slot = TPS * k + t
                            last = V.scalar_tensor_tensor(out=hc[:, t, :], in0=pacc[:, slot, :], scalar=rs["i"][:, slot:slot + 1],
                                                          in1=bin_row[:, :], op0=ALU.mult, op1=ALU.add)
                        last.then_inc(i_h, 1)
                    if layers:
                        if k < 2:
                            dve.wait_ge(i_h, 2 * p + k + 1)
                        else:
                            dve.wait_ge(f_h, u - 1)
                        norm_stats("c", lambda t: hc[:, t, :], TPS, DIM, c_st, c_mv, u)
                    if ffn:
                        dve.wait_ge(c_h, uf + 1)
                        norm_stats("f", lambda t: hf[:, t, :], TPS, DIM, f_st, f_mv, uf)
                    if layers:
                        dve.wait_ge(c_rs, u + 1)
                        after(dve, c_zT, u)
                        normalise("c", cz, hc).then_inc(c_z, 1)
                    if ffn:
                        dve.wait_ge(f_rs, uf + 1)
                        after(dve, f_zT, uf)
                        normalise("f", fz, hf).then_inc(f_z, 1)
                    if r.last((k - 1) % STEPS) if k else r.n >= 1:
                        v, s = (2 * p - 2, 0) if k == 0 else (2 * p - 1, 1)
                        if k < 2:
                            dve.wait_ge(l_zh, v + 1)
                            V.scalar_tensor_tensor(out=lzl[s][:, :], in0=F1[0][:, :], scalar=ZUP, in1=lzh[s][:, :],
                                                   op0=ALU.mult, op1=ALU.subtract).then_inc(l_zl, 1)
                    if r.end_late(k):
                        te = tau - 2
                        dve.wait_ge(e_mm, 2 * te + 2)
                        after(dve, s_out_b, 16 * te)
                        V.scalar_tensor_tensor(out=oh[:, :], in0=FO[:, HV:VOCAB], scalar=wds[:, 0:1], in1=h2[k % 2][:, HV:VOCAB],
                                               op0=ALU.mult, op1=ALU.add).then_inc(e_out, 1)
                    if end:
                        dve.wait_ge(e_wo, tau + 1)
                        if not (r.n == 1 and k < 2):
                            dve.wait_ge(s_out[k % 2], 16 * ((STEPS // 2) * (p - 1) + k // 2))
                            dve.wait_ge(e_out, 2 * tau - 2)
                        dve.wait_ge(s_mv, tau + 1)
                        V.scalar_tensor_tensor(out=h2[k % 2], in0=FW[:, :], scalar=wds[:, 2:3], in1=H1[:, k, :],
                                               op0=ALU.mult, op1=ALU.add).then_inc(e_h2, 1)
                        dve.wait_ge(e_h2, tau + 1)
                        norm_stats("e", lambda t: h2[k % 2], 1, VOCAB, e_st, e_mv, tau)
                    if ffn:
                        dve.wait_ge(f_zh, uf + 1)
                        after(dve, f_f1, 4 * uf)
                        V.scalar_tensor_tensor(out=fzl[:, :], in0=TF[:, :], scalar=ZUP, in1=fzh[:, :],
                                               op0=ALU.mult, op1=ALU.subtract).then_inc(f_zl, 1)
                    if layers:
                        V.tensor_tensor(H1[:, k, :], G[:, k, :], bo_row[:, :], ALU.add).then_inc(s_mv, 1)
                    if layers:
                        rb = rad[:, L:L + 1].to_broadcast([P, SEQ])
                        for n, (src, dst, u0) in enumerate(((cxc, cur, u0r), (cxs, cui, u0i))):
                            dve.wait_ge(c_rot, 2 * u + n + 1)
                            V.tensor_tensor_scan(dst, rb, src, u0[:, L:L + 1], ALU.mult, ALU.add).then_inc(c_scan, 1)
                    if end:
                        dve.wait_ge(e_rs, tau + 1)
                        after(dve, e_zl, tau)
                        V.tensor_scalar(ez, h2[k % 2], mv["e"][:, 0, 0:1], rs["e"][:, 0:1], ALU.subtract, ALU.mult).then_inc(e_z, 1)
                    if layers:
                        for n, (src, dst, tab) in enumerate(((cur, cxc, cosT), (cui, cxs, sinT))):
                            dve.wait_ge(c_scan, 2 * u + n + 1)
                            V.scalar_tensor_tensor(out=dst, in0=src, scalar=pcol("sc_lin", L), in1=tab[:, L, :],
                                                   op0=ALU.mult, op1=ALU.mult).then_inc(c_prod, 1)
                        dve.wait_ge(c_prod, 2 * u + 2)
                        V.tensor_tensor(cy, cxc, cxs, ALU.add).then_inc(c_y, 1)
                    if end:
                        dve.wait_ge(e_zh, tau + 1)
                        after(dve, e_T, 2 * tau)
                        V.scalar_tensor_tensor(out=ezl, in0=ez, scalar=ZUP, in1=ezh, op0=ALU.mult, op1=ALU.subtract).then_inc(e_zl, 1)
                    if r.end_mm(k):
                        tp = tau - 1
                        dve.wait_ge(e_mm, 2 * tp + 1)
                        hb = h2[(k - 1) % 2][:, 0:HV]
                        V.scalar_tensor_tensor(out=hb, in0=FO[:, 0:HV], scalar=wds[:, 0:1], in1=hb, op0=ALU.mult, op1=ALU.add).then_inc(e_out, 1)
                    if r.stats(k) and k >= 2:
                        tile_stats((6 + k) % STEPS, STEPS * p + 6 + k)
                    if layers:
                        dve.wait_ge(c_yT, u + 1)
                        V.tensor_tensor(flat(hc), flat(hc), TC[:, :], ALU.add).then_inc(c_h, 1)
                    if ffn:
                        dve.wait_ge(f_yT, uf + 1)
                        V.tensor_tensor(flat(hf), flat(hf), TF[:, :], ALU.add).then_inc(f_h, 1)
                    if r.last(k):
                        v, s = (2 * p, 0) if k == 7 else (2 * p - 1, 1)
                        dve.wait_ge(f_h, uf + 1)
                        norm_stats("l", lambda t: h[s][:, t, :], TPS, DIM, l_st, l_mv, v)
                        dve.wait_ge(l_rs, v + 1)
                        normalise("l", fy, h[s]).then_inc(l_z, 1)
            rounds(dve, body)


def kernel(x, L0_tok_W, L0_tok_b, L0_attn_Win, L0_attn_bin, L0_attn_ln1_w, L0_attn_ln1_b, L0_attn_phz_re,
           L0_attn_phz_im, L0_attn_lc_re, L0_attn_lc_im, L0_attn_sc_lin, L0_attn_ln2_w, L0_attn_ln2_b, L0_attn_W1,
           L0_attn_b1, L0_attn_W2, L0_attn_b2, L0_attn_lnl_w, L0_attn_lnl_b, L0_attn_Wout, L0_attn_bout, L0_ffn_W,
           L0_ffn_bias, L0_ffn_A, L0_ffn_Bf, L0_ffn_coeffs, L0_ffn_scales):
    import numpy as np
    import concourse.bacc as bacc
    from concourse.bass_utils import run_bass_kernel_spmd

    a = lambda v: np.asarray(v)
    c = np.ascontiguousarray
    xs = a(x)
    ctxs = np.stack([np.pad(xs, ((0, 0), (s, 0)), constant_values=VOCAB)[:, :SEQ] for s in (3, 2, 1, 0, 0)], -1)
    idx = c(ctxs.reshape(TILES, P, ORDER + 1).transpose(1, 0, 2))
    per_ch = lambda v, n: a(v).reshape(n, P).T
    parts = {
        "ln1_w": per_ch(L0_attn_ln1_w, 4), "ln1_b": per_ch(L0_attn_ln1_b, 4), "phz_re": per_ch(L0_attn_phz_re, 4),
        "phz_im": per_ch(L0_attn_phz_im, 4), "lc_re": per_ch(L0_attn_lc_re, 4), "lc_im": per_ch(L0_attn_lc_im, 4),
        "sc_lin": per_ch(L0_attn_sc_lin, 4), "ln2_w": per_ch(L0_attn_ln2_w, 4), "ln2_b": per_ch(L0_attn_ln2_b, 4),
        "b2": per_ch(L0_attn_b2, 4), "b1": per_ch(L0_attn_b1, 16), "lnl_w": per_ch(L0_attn_lnl_w, 1),
        "lnl_b": per_ch(L0_attn_lnl_b, 1), "tok_b": per_ch(L0_tok_b, 8),
        "coeffs": np.repeat(a(L0_ffn_coeffs), 16).reshape(2, P).T, "scales": np.repeat(a(L0_ffn_scales), 16).reshape(2, P).T,
    }
    cols = c(np.concatenate([parts[n] for n in PCOLS], 1))
    chunks = lambda m: c(m.reshape(-1, P, m.shape[-1]).transpose(1, 0, 2))
    W1 = a(L0_attn_W1)
    arrays = {
        "idx": idx, "tok_wt": c(a(L0_tok_W).T), "tok_w": c(a(L0_tok_W)), "cols": cols, "tok_b": c(a(L0_tok_b)),
        "win": c(a(L0_attn_Win)), "bin": c(a(L0_attn_bin)),
        "w1t": c(W1.transpose(2, 0, 1).reshape(P, DEPTH * DFF)),
        "w2t": c(a(L0_attn_W2).transpose(0, 2, 1).reshape(DEPTH, DFF // P, P, DIM).transpose(2, 0, 1, 3)),
        "woutt": c(a(L0_attn_Wout).T), "bout": c(a(L0_attn_bout)), "ffn_wt": chunks(a(L0_ffn_W).T), "ffn_bias": c(a(L0_ffn_bias)),
        "lora_a": chunks(a(L0_ffn_A).reshape(EXP, VOCAB)),
        "lora_bt": chunks(c(a(L0_ffn_Bf).transpose(0, 2, 1)).reshape(EXP, VOCAB)),
    }
    nc = bacc.Bacc("TRN2", target_bir_lowering=False, num_devices=1)
    args = [nc.dram_tensor(n, v.shape, mybir.dt.from_np(v.dtype), kind="ExternalInput").ap() for n, v in arrays.items()]
    out = nc.dram_tensor("out", (NSEQ * SEQ, VOCAB), mybir.dt.float32, kind="ExternalOutput").ap()
    ptab = nc.dram_tensor("ptab", (ROWS, DIM), mybir.dt.float32, kind="Internal").ap()
    tok3 = nc.dram_tensor("tok3", (VOCAB, VOCAB), mybir.dt.float32, kind="Internal").ap()
    program(nc, *args, out, ptab, tok3)
    r = run_bass_kernel_spmd(nc, [arrays], core_ids=[0])
    return r.results[0]["out"].reshape(NSEQ, SEQ, VOCAB)
```

```python
import concourse.bass as bass
from concourse import mybir
from contextlib import ExitStack

P = 128
ABSMAX = bass.bass_isa.ReduceOp.absmax
VOCAB, DIM, DFF, DEPTH = 1024, 128, 512, 4
NSEQ, SEQ = 16, 512
ORDER = 4
EXP = 16 * 16
TILES = NSEQ * SEQ // P
TPS = SEQ // P
STEPS = 2 * TPS
ROUNDS = NSEQ // 2
ROWS = ORDER * (VOCAB + 1)
EPS = 1e-5
ZUP = 256.0
WUP = 4096.0
PCOLS = {}
_at = 0
for _n, _w in (("ln1_w", 4), ("ln1_b", 4), ("phz_re", 4), ("phz_im", 4), ("lc_re", 4), ("lc_im", 4),
               ("sc_lin", 4), ("ln2_w", 4), ("ln2_b", 4), ("b2", 4), ("b1", 16), ("lnl_w", 1),
               ("lnl_b", 1), ("tok_b", 8), ("coeffs", 2), ("scales", 2)):
    PCOLS[_n] = (_at, _w)
    _at += _w
PWIDTH = _at


def program(nc, idx, tok_wt, tok_w, cols, tok_b, win, bin_, w1t, w2t, woutt, bout, ffn_wt, ffn_bias,
            lora_a, lora_bt, out, ptab):
    f32, f16, bf16, i32 = mybir.dt.float32, mybir.dt.float16, mybir.dt.bfloat16, mybir.dt.int32
    u32 = mybir.dt.uint32
    ALU, ACT, AX = mybir.AluOpType, mybir.ActivationFunctionType, mybir.AxisListType
    HV = VOCAB // 2
    VC = VOCAB // P
    FC = DFF // P
    KC = EXP // P

    ctx = ExitStack()
    with ctx:
        def sb(name, shape, dt=f32):
            return ctx.enter_context(nc.sbuf_tensor(name, shape, dt))

        def pb(name, shape, dt=f32):
            return ctx.enter_context(nc.psum_tensor(name, shape, dt))

        def sem(name):
            return ctx.enter_context(nc.semaphore(name))

        ident = sb("ident", [P, P])
        sc_parts = sb("sc_parts", [P, P], bf16)
        par = sb("par", [P, PWIDTH])
        idx_sb = sb("idx_sb", [P, TILES, ORDER], i32)
        idx_now = sb("idx_now", [P, ORDER], i32)
        idx_first = sb("idx_first", [P, STEPS, ORDER], i32)
        eps_t = sb("eps_t", [P, TPS])
        mhalf = sb("mhalf", [P, TPS])
        w1h = sb("w1h", [P, DEPTH * DFF], f16)
        w1l = sb("w1l", [P, DEPTH * DFF], f16)
        w2 = sb("w2", [P, DEPTH, FC, DIM])
        woh = sb("woh", [P, VOCAB], f16)
        wol = sb("wol", [P, VOCAB], f16)
        we = sb("we", [P, VC, 2, VOCAB], f16)
        bias_parts = sb("bias_parts", [P, VOCAB], bf16)
        cosT = sb("cosT", [P, DEPTH, SEQ])
        sinT = sb("sinT", [P, DEPTH, SEQ])
        b1p = sb("b1p", [P, DEPTH * FC])
        bo_row = sb("bo_row", [P, VOCAB])
        bin_row = sb("bin_row", [P, DIM])
        sm = sb("sm", [P, 128])
        G = sb("G", [P, STEPS, VOCAB])
        H1 = sb("H1", [P, STEPS, VOCAB])
        pacc = sb("pacc", [P, STEPS, DIM])
        h = [sb("hA", [P, TPS, DIM]), sb("hB", [P, TPS, DIM])]
        conv = sb("conv", [P, 6, SEQ])
        cz, cx, cxc, cxs, cur, cui = (conv[:, n, :] for n in range(6))
        cy = cx
        fz = sb("fz", [P, SEQ])
        fzh = sb("fzh", [P, SEQ], f16)
        fzl = sb("fzl", [P, SEQ], f16)
        fg = sb("fg", [P, FC, SEQ])
        fy = sb("fy", [P, SEQ])
        lzf = sb("lzf", [P, P])
        lzh = [sb("lzhA", [P, SEQ], f16), sb("lzhB", [P, SEQ], f16)]
        lzl = [sb("lzlA", [P, SEQ], f16), sb("lzlB", [P, SEQ], f16)]
        AR = sb("AR", [P, 3 * VOCAB])
        tokb_row = sb("tokb_row", [P, VOCAB])
        h2 = [AR[:, 0:VOCAB], AR[:, VOCAB:2 * VOCAB]]
        ez = AR[:, 2 * VOCAB:3 * VOCAB]
        ezT = [sb("ezT0", [P, 2, VOCAB], f16), sb("ezT1", [P, 2, VOCAB], f16)]
        oh = sb("oh", [P, HV])
        st = {n: sb("st_" + n, [P, TPS, 12]) for n in "cfle"}
        mv = {n: sb("mv_" + n, [P, TPS, 2]) for n in "cfle"}
        ve = {n: sb("ve_" + n, [P, TPS]) for n in "cfle"}
        rs = {n: sb("rs_" + n, [P, TPS]) for n in "cfle"}
        nm = sb("nm", [P, TPS])
        st["i"], mv["i"] = sb("st_i", [P, STEPS, 12]), sb("mv_i", [P, STEPS, 2])
        ve["i"], rs["i"] = sb("ve_i", [P, STEPS]), sb("rs_i", [P, STEPS])

        TC = pb("TC", [P, SEQ])
        TF = pb("TF", [P, SEQ])
        F1 = [pb("F1a", [P, SEQ]), pb("F1b", [P, SEQ])]
        FO = pb("FO", [P, VOCAB])
        FW = pb("FW", [P, VOCAB])

        wblk = [[H1[:, 4 * b + 2 * n:4 * b + 2 * n + 2, :].rearrange("p a b -> p (a b)").rearrange("p (v j) -> p v j", v=4)
                 for n in range(2)] for b in range(2)]
        ptT = [fg[:, n, :] for n in range(2)]
        pt_rows = [fz[:, :].rearrange("p (t d) -> p t d", t=4), fy[:, :].rearrange("p (t d) -> p t d", t=4)]
        win_sb = conv[:, 4:6, :].rearrange("p a b -> p (a b)")
        winT = ezT[0][:, :, :].rearrange("p a b -> p (a b)").bitcast(f32).rearrange("p (v d) -> p v d", v=VC)
        w1f = w2[:, :, :, :].rearrange("p a b c -> p (a b c)")
        la = AR[:, 0:2 * VOCAB].rearrange("p (k i) -> p k i", k=KC)
        lb = [AR[:, 2 * VOCAB:3 * VOCAB], ezT[1][:, :, :].rearrange("p a b -> p (a b)").bitcast(f32)]
        wsum = [ezT[0][:, :, :].rearrange("p a b -> p (a b)").bitcast(f32), H1[:, STEPS - 1, :]]
        tmp = [conv[:, 2 * n:2 * n + 2, :].rearrange("p a b -> p (a b)").rearrange("p (l m) -> p l m", l=DEPTH) for n in range(2)]
        lnlb = lzf[:, :]
        weff = we[:, :, :, :].rearrange("p v h o -> p (v h o)").bitcast(f32).rearrange("p (v o) -> p v o", v=VC)
        wof, bfs, bh = weff[:, 0, :], weff[:, 1, :], weff[:, 2, 0:HV].bitcast(bf16)

        def S(n, w=DEPTH):
            return sm[:, n:n + w]
        mag2, mag, rad, inv, cs1, sn1, t1, t2, t3, u0r, u0i = (S(4 * n) for n in range(11))
        cm, sm_ = S(44), S(48)
        wmax, wsc, wds = S(52, 3), S(56, 3), S(60, 3)
        bp4, lw = S(64, 1), S(66, 2)
        wmaxp = S(70, 3)
        stw, mvw = S(74, 12), S(86, 2)
        t4 = S(88)
        dmax, dmaxp, wpart = S(92, 3), S(96, 3), S(100, 4)
        bmask, smask = S(104, 3), S(108, 3)
        sparts = S(112, 4)

        def pcol(name, n=0, w=1):
            return par[:, PCOLS[name][0] + n:PCOLS[name][0] + n + w]

        s_par, s_idx, s_rows, s_win, s_w1, s_wo, s_w2, s_weff, s_lora, s_bo = (
            sem(n) for n in ("par_in", "idx_in", "rows_in", "win_in", "w1_in", "wo_in", "w2_in",
                             "ffnw_in", "lora_in", "bout_in"))
        s_wblk = [[sem("wblk_in%d%d" % (b, n)) for n in range(2)] for b in range(2)]
        s_tb, s_bf = sem("tok_b_in"), sem("ffn_bias_in")
        s_const = sem("consts")
        s_idx2 = sem("idx_offset")
        s_dv = sem("dve_setup")
        s_lo_chain = sem("vector_setup_chain")
        s_pl = sem("pool_setup")
        s_rad = sem("radius")
        s_pmag = sem("magnitude")
        s_winc, s_winp, s_winT, s_bpp, s_bp = (sem(n) for n in (
            "win_centred", "win_transposed", "win_t_copied", "bp_product", "bp_done"))
        s_ptp, s_pte, s_ptt, s_ptr = (sem(n) for n in (
            "ptab_product", "ptab_evacuated", "ptab_turned", "ptab_rows"))
        s_ptd = [sem("ptab_out0"), sem("ptab_out1")]
        s_ptl = sem("ptab_out_last")
        s_b1m, s_bom, s_lom = sem("b1_product"), sem("bo_product"), sem("lora_product")
        s_lbs, s_lad, s_max, s_red = sem("lora_b_weighted"), sem("lora_added"), sem("wmax_part"), sem("wmax_all")
        s_hi, s_lo, s_whi, s_wlo = sem("w_hi"), sem("w_lo"), sem("dense_hi"), sem("dense_lo")
        s_fill = sem("g_filled")
        s_scaled = sem("w_scale")
        s_gT, s_gP = sem("g_token_sum"), sem("g_projected_sum")
        s_fT, s_fP = ([sem("first_%s_sum%d" % (n, q)) for q in range(2)] for n in ("token", "projected"))
        s_ix, s_mv = sem("idx_now_ready"), sem("h1_moved")
        i_st, i_mv, i_ve, i_rs, i_h = (sem("in_" + n) for n in ("stats", "meanvar", "vareps", "rstd", "h"))
        c_st, c_mv, c_ve, c_rs, c_z, c_zT, c_x, c_rot, c_scan, c_prod, c_y, c_yT, c_h = (sem("conv_" + n) for n in (
            "stats", "meanvar", "vareps", "rstd", "z", "zT", "x", "rot", "scan", "prod", "y", "yT", "h"))
        f_st, f_mv, f_ve, f_rs, f_z, f_zT, f_zh, f_zl, f_f1, f_g, f_f2, f_y, f_yT, f_h = (sem("ffn_" + n) for n in (
            "stats", "meanvar", "vareps", "rstd", "z", "zT", "zh", "zl", "f1", "g", "f2", "y", "yT", "h"))
        l_nm = sem("last_shift")
        l_st, l_mv, l_ve, l_rs, l_z, l_zT, l_zh, l_zl = (sem("last_" + n) for n in (
            "stats", "meanvar", "vareps", "rstd", "z", "zT", "zh", "zl"))
        e_wo, e_h2, e_st, e_mv, e_ve, e_rs, e_z, e_zh, e_zl, e_T, e_mm, e_out = (sem("end_" + n) for n in (
            "wo", "h2", "stats", "meanvar", "vareps", "rstd", "z", "zh", "zl", "turned", "mm", "out"))
        s_out = [sem("out_dma0"), sem("out_dma1")]
        s_out_b = sem("out_dma_second_half")

        def after(eng, s, v):
            if not (isinstance(v, int) and v <= 0):
                eng.wait_ge(s, v)

        def held(eng, v):
            return v if isinstance(v, int) else eng.to_reg(v)

        class Round:
            def __init__(self, p):
                n = p if isinstance(p, int) else 3
                self.p = p
                self.layers = n < ROUNDS
                self.first, self.n = n == 0, n

            def lora(self, k):
                return 2 * (k - 3) if self.first and 3 <= k < 3 + VC // 2 else None

            def ffn(self, k):
                return 0 <= STEPS * self.n + k - 1 < STEPS * ROUNDS

            def end(self, k):
                return self.n >= 1 and k < STEPS

            def end_mm(self, k):
                return 0 <= STEPS * (self.n - 1) + k - 1 < TILES

            def end_late(self, k):
                return 0 <= STEPS * (self.n - 1) + k - 2 < TILES

            def gather(self, k):
                return STEPS <= STEPS * self.n + 7 + k < TILES

            def stats(self, k):
                return STEPS <= STEPS * self.n + 6 + k < TILES

            def stats_at(self, k):
                return [n for n in ((0, 1), (), *((m,) for m in range(2, STEPS)))[k] if self.stats(n)] if k < STEPS else []

            def last(self, k):
                return k < 2 and self.n >= 1

            def ffn_first(self, k):
                return k == 1 and self.n >= 1 and self.layers

            def steps(self):
                return STEPS + 2 if self.n == ROUNDS else STEPS

        def rounds(eng, body):
            body(Round(0))
            body(Round(1))
            with eng.Fori(2, ROUNDS - 1) as p:
                body(Round(p))
            body(Round(ROUNDS - 1))
            body(Round(ROUNDS))

        block = ctx.enter_context(nc.Block())

        @block.sync
        def _(sp):
            tokv = tok_w.rearrange("(v p) j -> p v j", p=P)

            def block_in(b):
                n = 512 if b < 8 else ROWS - 8 * 512
                for half in range(2):
                    if b >= 2:
                        sp.wait_ge(s_ptp, 2 * (b - 2) + half + 1)
                    sp.dma_start(wblk[b % 2][half][:, :, 0:n], tokv[:, 4 * half:4 * half + 4, 512 * b:512 * b + n]).then_inc(s_wblk[b % 2][half], 16)

            sp.dma_start(par[:, :], cols).then_inc(s_par, 16)
            sp.dma_start(win_sb, win).then_inc(s_win, 16)
            block_in(0)
            sp.dma_start(tokb_row[:, :], tok_b.partition_broadcast(P)).then_inc(s_tb, 16)
            sp.dma_start(idx_sb[:, :, :], idx).then_inc(s_idx, 16)
            sp.dma_start(bin_row[:, :], bin_.partition_broadcast(P)).then_inc(s_rows, 16)
            sp.dma_start(bfs, ffn_bias.partition_broadcast(P)).then_inc(s_bf, 16)
            sp.dma_start(w1f, w1t).then_inc(s_w1, 16)
            block_in(1)
            sp.dma_start(wof, woutt).then_inc(s_wo, 16)
            sp.dma_start(bo_row[:, :], bout.partition_broadcast(P)).then_inc(s_bo, 16)
            for b in range(2, 9):
                block_in(b)
            sp.wait_ge(s_fP[0], 16 * TPS * ORDER)
            sp.wait_ge(s_lo, 1)
            sp.dma_start(w2[:, :, :, :], w2t).then_inc(s_w2, 16)
            sp.wait_ge(s_fT[1], 16 * TPS * 2)
            sp.dma_start(la, lora_a).then_inc(s_lora, 16)
            for q in range(KC):
                sp.dma_start(lb[q], lora_bt[:, q, :]).then_inc(s_lora, 16)
            sp.wait_ge(s_lo, 2)
            sp.wait_ge(s_fT[1], 16 * TPS * ORDER)
            for v in range(0, VC, 2):
                sp.dma_start(weff[:, v:v + 2, :], ffn_wt[:, v:v + 2, :]).then_inc(s_weff, 16)

            def body(r):
                for k in range(r.steps()):
                    if r.end_late(k):
                        tau = STEPS * (r.p - 1) + k - 2
                        sp.wait_ge(e_out, 2 * tau + 2)
                        sp.dma_start(out[bass.ds(tau * P, P), HV:VOCAB], oh[:, :]).then_inc(s_out_b, 16)
                    if r.end_mm(k):
                        tau = STEPS * (r.p - 1) + k - 1
                        sp.wait_ge(e_out, 2 * tau + 1)
                        sp.dma_start(out[bass.ds(tau * P, P), 0:HV], h2[(k - 1) % 2][:, 0:HV]).then_inc(s_out[(k - 1) % 2], 16)
            rounds(sp, body)
            sp.wait_ge(s_out[0], 16 * TILES // 2)
            sp.wait_ge(s_out[1], 16 * TILES // 2)
            sp.wait_ge(s_out_b, 16 * TILES)
            for b in range(2):
                sp.wait_ge(s_ptd[b], 64)
            sp.wait_ge(s_ptl, 16)

        @block.gpsimd
        def _(pool):
            nc.gpsimd.memset(ident[:, :], 0.0).then_inc(s_pl, 1)
            nc.gpsimd.memset(eps_t[:, :], EPS)
            nc.gpsimd.memset(mhalf[:, :], -0.5).then_inc(s_const, 1)
            pool.wait_ge(s_pl, 1)
            nc.gpsimd.affine_select(out=ident[:, :], in_=ident[:, :], compare_op=ALU.not_equal, fill=1.0, base=0,
                                    pattern=[[-1, P]], channel_multiplier=1).then_inc(s_const, 1)

            def gather_tok(slot, ix, k, done=s_gT):
                nc.gpsimd.indirect_dma_start(G[:, slot, :], None, tok_wt, bass.IndirectOffsetOnAxis(ap=ix[:, k:k + 1].bitcast(u32), axis=0),
                                             compute_op=ALU.add).then_inc(done, 16)

            def gather_proj(slot, ix, first, rows=ROWS, done=s_gP):
                nc.gpsimd.indirect_dma_start(pacc[:, slot, :], None, ptab[0:rows, :], bass.IndirectOffsetOnAxis(ap=ix.bitcast(u32), axis=0),
                                             compute_op=ALU.bypass if first else ALU.add).then_inc(done, 16)

            nc.gpsimd.memset(t4, 0.5).then_inc(s_pl, 1)
            pool.wait_ge(s_pl, 2)
            pool.wait_ge(s_dv, 1)
            nc.gpsimd.tensor_tensor(mag, mag2, t4, ALU.pow).then_inc(s_pmag, 1)
            pool.wait_ge(s_idx2, 4)
            nc.gpsimd.tensor_copy(idx_first[:, :, :], idx_sb[:, 0:STEPS, :]).then_inc(s_pl, 1)
            pool.wait_ge(s_pl, 3)

            def first_tokens(s, k):
                if k == 0:
                    pool.wait_ge(s_fill, TPS * (s + 1))
                after(pool, s_fT[s], 16 * TPS * k)
                for t in range(TPS * s, TPS * s + TPS):
                    gather_tok(t, idx_first[:, t, :], k, s_fT[s])

            def first_projected(s, k):
                last = ((k + 1) * (VOCAB + 1) - 1) // 512
                pool.wait_ge(s_ptd[0], 16 * min(last // 2 + 1, 4))
                pool.wait_ge(s_ptd[1], 16 * min((last + 1) // 2, 4))
                if last == 8:
                    pool.wait_ge(s_ptl, 16)
                after(pool, s_fP[s], 16 * TPS * k)
                for t in range(TPS * s, TPS * s + TPS):
                    gather_proj(t, idx_first[:, t, k:k + 1], k == 0, (k + 1) * (VOCAB + 1), s_fP[s])

            def rstd(n, tiles, mvsem, vesem, rssem, v, at=0):
                q = slice(at, at + tiles)
                pool.wait_ge(mvsem, v + 1)
                nc.gpsimd.tensor_tensor(ve[n][:, q], mv[n][:, q, 1], eps_t[:, 0:tiles], ALU.add).then_inc(vesem, 1)
                pool.wait_ge(vesem, v + 1)
                nc.gpsimd.tensor_tensor(rs[n][:, q], ve[n][:, q], mhalf[:, 0:tiles], ALU.pow).then_inc(rssem, 1)

            def first_projected_both(k):
                for s in range(2):
                    first_projected(s, k)

            first_tokens(0, 0)
            first_tokens(0, 1)
            first_tokens(0, 2)
            first_projected_both(0)
            first_tokens(0, 3)
            first_projected_both(1)
            for n in range(2):
                pool.wait_ge(s_max, n + 1)
                nc.gpsimd.partition_all_reduce(wmax[:, n + 1:n + 2], wmaxp[:, n + 1:n + 2], P, ABSMAX).then_inc(s_red, 1)
            first_tokens(1, 0)
            first_projected(0, 2)
            for t in range(TPS):
                rstd("i", 1, i_mv, i_ve, i_rs, t, t)
            first_projected(0, 3)
            first_tokens(1, 1)

            def body(r):
                p = r.p
                for k in range(STEPS):
                    def gather_round(kk):
                        if not r.gather(k):
                            return
                        tau, slot = STEPS * p + 7 + k, (7 + k) % STEPS
                        before = held(pool, 64 * (tau - STEPS) + 16 * kk)
                        if kk > 0:
                            pool.wait_ge(s_const, 2)
                        after(pool, s_gT, before)
                        after(pool, s_gP, before)
                        if kk == 0:
                            nc.gpsimd.tensor_copy(idx_now[:, :], idx_sb[:, bass.ds(tau, 1), :].rearrange("p a b -> p (a b)")).then_inc(s_ix, 1)
                            filled, used = held(pool, tau + 1), held(pool, 2 * (p if k else p - 1) + slot // TPS + 1)
                            copied = held(pool, tau - STEPS + 1)
                            pool.wait_ge(s_const, 2)
                            pool.wait_ge(s_ix, copied)
                            pool.wait_ge(s_fill, filled)
                            pool.wait_ge(i_h, used)
                        gather_tok(slot, idx_now[:, :], kk)
                        gather_proj(slot, idx_now[:, kk:kk + 1], kk == 0)

                    if k == 0:
                        gather_round(0)
                    if r.first and k == 1:
                        for t in range(TPS, STEPS):
                            rstd("i", 1, i_mv, i_ve, i_rs, t, t)
                    if r.layers:
                        rstd("c", TPS, c_mv, c_ve, c_rs, STEPS * p + k)
                    if r.ffn(k) and not r.ffn_first(k):
                        rstd("f", TPS, f_mv, f_ve, f_rs, STEPS * p + k - 1)
                    if k > 0:
                        gather_round(0)
                    if r.last(k):
                        rstd("l", TPS, l_mv, l_ve, l_rs, 2 * (p - 1) + k)
                    if r.first and k == 0:
                        first_projected(1, 2)
                    if r.layers:
                        u, L = STEPS * p + k, k // 2
                        pool.wait_ge(c_x, u + 1)
                        after(pool, c_y, u)
                        nc.gpsimd.tensor_tensor(cxc, cx, cosT[:, L, :], ALU.mult).then_inc(c_rot, 1)
                        nc.gpsimd.tensor_tensor(cxs, cx, sinT[:, L, :], ALU.mult).then_inc(c_rot, 1)
                    gather_round(1)
                    if k == 0:
                        gather_round(2)
                        for n in r.stats_at(k)[:1]:
                            rstd("i", 1, i_mv, i_ve, i_rs, STEPS * p + 6 + n, (6 + n) % STEPS)
                    if r.end(k):
                        rstd("e", 1, e_mv, e_ve, e_rs, STEPS * (p - 1) + k)
                    if k > 0:
                        gather_round(2)
                    gather_round(3)
                    if r.first and k == 0:
                        first_tokens(1, 2)
                        first_projected(1, 3)
                        first_tokens(1, 3)
                    if r.first and k == 2:
                        pool.wait_ge(s_max, 3)
                        nc.gpsimd.partition_all_reduce(dmax, dmaxp, P, ABSMAX).then_inc(s_red, 1)
                    if r.ffn_first(k + 1) and k == 0:
                        rstd("f", TPS, f_mv, f_ve, f_rs, STEPS * p + k)
                    for n in r.stats_at(k)[1:] if k == 0 else r.stats_at(k):
                        rstd("i", 1, i_mv, i_ve, i_rs, STEPS * p + 6 + n, (6 + n) % STEPS)
            rounds(pool, body)

        @block.scalar
        def _(act):
            act.wait_ge(s_winp, 1)
            nc.scalar.activation(winT.rearrange("p v d -> p (v d)"), FO[:, :], ACT.Copy).then_inc(s_winT, 1)
            act.wait_ge(s_pmag, 1)
            nc.scalar.activation(rad, mag, ACT.Tanh).then_inc(s_rad, 1)
            def fill(slot):
                nc.scalar.activation(G[:, slot, :], tokb_row[:, :], ACT.Copy).then_inc(s_fill, 1)

            act.wait_ge(s_tb, 16)
            for t in range(STEPS):
                fill(t)

            def high(dst, src, n):
                nc.scalar.activation(dst, src, ACT.Identity, scale=wsc[:, n:n + 1]).then_inc(s_hi, 1)

            def rows_copied(b):
                act.wait_ge(s_ptt, b + 1)
                if b >= 2:
                    act.wait_ge(s_ptd[b % 2], 16 * (b // 2))
                w = ROWS - 8 * 512
                if b < 8:
                    nc.scalar.activation(pt_rows[b % 2].rearrange("p t d -> p (t d)"), (TC, TF)[b % 2][:, :], ACT.Copy).then_inc(s_ptr, 1)
                    act.wait_ge(s_ptr, b + 1)
                    nc.scalar.dma_start(ptab[512 * b:512 * b + 512, :].rearrange("(t p) d -> p t d", p=P), pt_rows[b % 2]).then_inc(s_ptd[b % 2], 16)
                else:
                    nc.scalar.activation(pt_rows[0][0:w, 0, :], TC[0:w, 0:P], ACT.Copy).then_inc(s_ptr, 1)
                    act.wait_ge(s_ptr, 9)
                    nc.scalar.dma_start(ptab[8 * 512:ROWS, :], pt_rows[0][0:w, 0, :]).then_inc(s_ptl, 16)

            act.wait_ge(s_bp, 1)
            for b in range(9):
                n = 512 if b < 8 else ROWS - 8 * 512
                act.wait_ge(s_ptp, 2 * b + 2)
                if b >= 2:
                    act.wait_ge(s_ptt, b - 1)
                nc.scalar.activation(ptT[b % 2][:, 0:n], F1[b % 2][:, 0:n], ACT.Identity, bias=bp4).then_inc(s_pte, 1)
                if b >= 1:
                    rows_copied(b - 1)
            rows_copied(8)
            act.wait_ge(s_scaled, 1)
            high(w1h[:, :], w1f, 1)
            act.wait_ge(s_scaled, 2)
            high(woh[:, :], wof, 2)

            def dense_high(v):
                act.wait_ge(s_lad, v + 1)
                act.wait_ge(s_scaled, 3)
                nc.scalar.activation(we[:, v, 0, :], wsum[v % 2], ACT.Identity, scale=wsc[:, 0:1]).then_inc(s_whi, 1)

            def body(r):
                p = r.p
                for k in range(STEPS):
                    u, uf, tau, L, Lf = STEPS * p + k, STEPS * p + k - 1, STEPS * (p - 1) + k, k // 2, (k - 1) % STEPS // 2
                    def x_conv():
                        act.wait_ge(c_zT, u + 1)
                        after(act, c_yT, u)
                        nc.scalar.activation(cx, TC[:, :], ACT.Silu, bias=pcol("ln1_b", L), scale=pcol("ln1_w", L)).then_inc(c_x, 1)

                    if r.layers and not r.ffn_first(k):
                        x_conv()
                    if r.ffn(k):
                        act.wait_ge(f_zT, uf + 1)
                        after(act, f_f1, 4 * uf)
                        nc.scalar.activation(fzh[:, :], TF[:, :], ACT.Copy, scale=ZUP).then_inc(f_zh, 1)
                    if r.ffn_first(k):
                        x_conv()
                    if k > 0 and r.lora(k - 1) is not None:
                        dense_high(r.lora(k - 1) + 1)
                    if r.last(k):
                        act.wait_ge(l_nm, 2 * (p - 1) + k + 1)
                        for t in range(TPS):
                            o = fy[:, P * t:P * t + P]
                            last = nc.scalar.activation(o, o, ACT.Identity, bias=nm[:, t:t + 1], scale=rs["l"][:, t:t + 1])
                        last.then_inc(l_z, 1)

                    def last_high():
                        act.wait_ge(l_zT, 2 * (p - 1) + k + 1)
                        if r.n >= 2:
                            act.wait_ge(e_wo, STEPS * (p - 2) + TPS * (k + 1))
                        nc.scalar.activation(lzh[k][:, :], TC[:, :], ACT.Copy, scale=ZUP).then_inc(l_zh, 1)

                    if r.last(k) and not r.ffn_first(k):
                        last_high()
                    if r.ffn(k):
                        for c in range(FC):
                            if r.ffn_first(k) and c == 2:
                                last_high()
                            act.wait_ge(f_f1, 4 * uf + c + 1)
                            after(act, f_f2, uf)
                            nc.scalar.activation(fg[:, c, :], F1[c % 2][:, :], ACT.Silu, bias=b1p[:, FC * Lf + c:FC * Lf + c + 1],
                                                 scale=wds[:, 1:2]).then_inc(f_g, 1)
                    def end_high():
                        act.wait_ge(e_T, tau + 1)
                        after(act, e_mm, 2 * tau - 2)
                        nc.scalar.activation(ezT[k % 2][:, 0, :], FW[:, :], ACT.Copy, scale=ZUP).then_inc(e_zh, 1)

                    if r.end(k) and not (k == 0 or r.ffn_first(k)):
                        end_high()
                    if r.ffn(k):
                        act.wait_ge(f_f2, uf + 1)
                        after(act, f_yT, uf)
                        if r.last(k):
                            act.wait_ge(l_zT, 2 * (p - 1) + k + 1)
                        nc.scalar.activation(fy[:, :], TF[:, :], ACT.Identity, bias=pcol("b2", Lf)).then_inc(f_y, 1)
                    if r.end(k) and (k == 0 or r.ffn_first(k)):
                        end_high()
                    if r.lora(k) is not None:
                        dense_high(r.lora(k))
                    if r.n < ROUNDS - 1:
                        act.wait_ge(s_mv, u + 1)
                        fill(k)
            rounds(act, body)

        @block.tensor
        def _(pe):
            mm = nc.tensor.matmul

            def turn(dst, src, n):
                for t in range(n):
                    last = nc.tensor.transpose(dst[:, P * t:P * t + P], src[:, P * t:P * t + P], ident[:, :])
                return last

            pe.wait_ge(s_const, 2)
            pe.wait_ge(s_winc, 1)
            turn(FO, win_sb, VC).then_inc(s_winp, 1)
            pe.wait_ge(s_winT, 1)
            pe.wait_ge(s_par, 16)
            for v in range(VC):
                last = mm(TC[:, 0:1], winT[:, v, :], pcol("tok_b", v), start=v == 0, stop=v == VC - 1)
            last.then_inc(s_bpp, 1)

            pe.wait_ge(s_bp, 1)
            def bias_products():
                pe.wait_ge(s_w1, 16)
                for L in range(DEPTH):
                    for c in range(FC):
                        n = FC * L + c
                        last = mm(FO[:, n:n + 1], w1f[:, P * n:P * n + P], pcol("ln2_b", L), start=True, stop=True)
                last.then_inc(s_b1m, 1)
                pe.wait_ge(s_wo, 16)
                pe.wait_ge(s_dv, 3)
                for n in range(2):
                    last = mm(FW[:, n * HV:n * HV + HV], lnlb, wof[:, n * HV:n * HV + HV], start=True, stop=True)
                last.then_inc(s_bom, 1)

            def turn_block(b):
                pe.wait_ge(s_pte, b + 1)
                if b >= 2:
                    pe.wait_ge(s_ptr, b - 1)
                dst = (TC, TF)[b % 2]
                if b < 8:
                    turn(dst, ptT[b % 2], 4).then_inc(s_ptt, 1)
                else:
                    w = ROWS - 8 * 512
                    nc.tensor.transpose(dst[0:w, 0:P], ptT[b % 2][:, 0:w], ident[:, :]).then_inc(s_ptt, 1)

            for b in range(9):
                n = 512 if b < 8 else ROWS - 8 * 512
                if b >= 2:
                    pe.wait_ge(s_pte, b - 1)
                for half in range(2):
                    pe.wait_ge(s_wblk[b % 2][half], 16 * (b // 2 + 1))
                    for v in range(4):
                        last = mm(F1[b % 2][:, 0:n], winT[:, 4 * half + v, :], wblk[b % 2][half][:, v, 0:n],
                                  start=half == 0 and v == 0, stop=half == 1 and v == 3)
                    last.then_inc(s_ptp, 1)
                if b >= 1:
                    turn_block(b - 1)
                if b == 1:
                    bias_products()
            turn_block(8)
            pe.wait_ge(s_ptr, 9)
            pe.wait_ge(s_lo, 2)

            def split3(dst, wh, wl, ah, al, start, stop):
                mm(dst, wh, ah, start=start, stop=False)
                mm(dst, wl, ah, start=False, stop=False)
                return mm(dst, wh, al, start=False, stop=stop)

            def lora(v):
                pe.wait_ge(s_lora, 16 * (1 + KC))
                pe.wait_ge(s_lbs, 1)
                after(pe, s_lad, v)
                for n in range(2):
                    for q in range(KC):
                        last = mm(FO[:, n * HV:n * HV + HV], la[:, q, P * v:P * v + P], lb[q][:, n * HV:n * HV + HV],
                                  start=q == 0, stop=q == KC - 1)
                last.then_inc(s_lom, 1)

            def body(r):
                p = r.p
                for k in range(STEPS + 1 if r.n == ROUNDS else STEPS):
                    u, uf, tau, Lf = STEPS * p + k, STEPS * p + k - 1, STEPS * (p - 1) + k, (k - 1) % STEPS // 2
                    def project():
                        s, t = k // TPS, k % TPS
                        pe.wait_ge(l_zl, 2 * (p - 1) + s + 1)
                        after(pe, e_zh, tau)
                        after(pe, e_zl, tau)
                        for n in range(2):
                            o = slice(n * HV, n * HV + HV)
                            mm(FW[:, o], lzh[s][:, P * t:P * t + P], woh[:, o], start=True, stop=False)
                            mm(FW[:, o], lzh[s][:, P * t:P * t + P], wol[:, o], start=False, stop=False)
                            last = mm(FW[:, o], lzl[s][:, P * t:P * t + P], woh[:, o], start=False, stop=True)
                        last.then_inc(e_wo, 1)

                    def z_conv():
                        pe.wait_ge(c_z, u + 1)
                        after(pe, c_h, u)
                        turn(TC, cz, TPS).then_inc(c_zT, 1)

                    def z_ffn():
                        pe.wait_ge(f_z, uf + 1)
                        after(pe, f_h, uf)
                        turn(TF, fz, TPS).then_inc(f_zT, 1)

                    def z_last():
                        v = 2 * (p - 1) + k
                        pe.wait_ge(l_z, v + 1)
                        if r.layers:
                            pe.wait_ge(c_x, u + 1)
                        elif k == 1:
                            pe.wait_ge(l_zl, v)
                        else:
                            pe.wait_ge(c_h, u)
                        turn(TC, fy, TPS).then_inc(l_zT, 1)

                    def end_half(n, v0=0, v1=VC):
                        tp = tau - 1
                        o = slice(n * HV, n * HV + HV)
                        if v0 == 0:
                            if n == 0:
                                if r.n == 1 and k == 1:
                                    pe.wait_ge(s_wlo, VC)
                                pe.wait_ge(e_zh, tp + 1)
                                pe.wait_ge(e_zl, tp + 1)
                            after(pe, e_out, 2 * tp - 1 + n)
                            mm(FO[:, o], sc_parts[:, :], bias_parts[:, o], start=True, stop=False)
                        for v in range(v0, v1):
                            zT = ezT[(k - 1) % 2]
                            zh, zl = zT[:, 0, P * v:P * v + P], zT[:, 1, P * v:P * v + P]
                            mm(FO[:, o], zh, we[:, v, 0, o], start=False, stop=False)
                            mm(FO[:, o], zh, we[:, v, 1, o], start=False, stop=False)
                            last = mm(FO[:, o], zl, we[:, v, 0, o], start=False, stop=v == VC - 1)
                        if v1 == VC:
                            last.then_inc(e_mm, 1)

                    def up(c):
                        after(pe, f_g, 4 * uf + c - 1)
                        w = slice(DFF * Lf + P * c, DFF * Lf + P * c + P)
                        split3(F1[c % 2][:, :], w1h[:, w], w1l[:, w], fzh[:, :], fzl[:, :], True, True).then_inc(f_f1, 1)

                    def z_end():
                        pe.wait_ge(e_z, tau + 1)
                        turn(FW, ez, VC).then_inc(e_T, 1)

                    def down(c):
                        pe.wait_ge(f_g, 4 * uf + c + 1)
                        return mm(TF[:, :], w2[:, Lf, c, :], fg[:, c, :], start=c == 0, stop=c == FC - 1)

                    if r.end(k) and k > 0:
                        project()
                    dense = r.end_mm(k)
                    if r.ffn_first(k):
                        z_ffn()
                    if dense and r.last(k):
                        end_half(0, 0, VC if r.ffn_first(k) else VC // 2)
                    if r.layers:
                        z_conv()
                    if r.ffn(k) and not r.ffn_first(k):
                        z_ffn()
                    if dense and not r.ffn_first(k):
                        end_half(0, VC // 2 if r.last(k) else 0)
                    if r.last(k) and not r.ffn_first(k):
                        z_last()
                    if r.lora(k) is not None:
                        lora(r.lora(k))
                    if r.first and k == 1:
                        pe.wait_ge(s_w2, 16)
                    if r.ffn(k):
                        pe.wait_ge(f_zl, uf + 1)
                        up(0)
                        up(1)
                        if r.ffn_first(k):
                            z_last()
                        if r.end(k) and not r.last(k):
                            z_end()
                        up(2)
                        down(0)
                        if r.end(k) and k == 0:
                            project()
                        up(3)
                        down(1)
                        down(2)
                        down(3).then_inc(f_f2, 1)
                        if r.ffn_first(k):
                            z_end()
                    elif r.end(k):
                        if k == 0:
                            project()
                        z_end()
                    if r.layers:
                        pe.wait_ge(c_y, u + 1)
                        if r.last(k):
                            pe.wait_ge(l_zl, 2 * (p - 1) + k + 1)
                        turn(TC, cy, TPS).then_inc(c_yT, 1)
                    if dense:
                        end_half(1, 0, 1)
                    if r.ffn(k):
                        pe.wait_ge(f_y, uf + 1)
                        turn(TF, fy, TPS).then_inc(f_yT, 1)
                    if r.ffn(k) and r.end(k) and k == 0:
                        if dense:
                            end_half(1, 1, 3)
                        z_end()
                        if dense:
                            end_half(1, 3)
                    elif dense:
                        end_half(1, 1)
                    if r.lora(k) is not None:
                        lora(r.lora(k) + 1)
            rounds(pe, body)

        @block.vector
        def _(dve):
            V = nc.vector
            done = [0]

            def chain(ins):
                done[0] += 1
                ins.then_inc(s_lo_chain, 1)
                dve.wait_ge(s_lo_chain, done[0])

            dve.wait_ge(s_par, 16)
            chain(V.tensor_tensor(t1, pcol("phz_re", 0, 4), pcol("phz_re", 0, 4), ALU.mult))
            chain(V.tensor_tensor(t2, pcol("phz_im", 0, 4), pcol("phz_im", 0, 4), ALU.mult))
            V.tensor_tensor(mag2, t1, t2, ALU.add).then_inc(s_dv, 1)
            dve.wait_ge(s_win, 16)
            chain(V.bn_stats(stw[:, 0:6], win_sb[:, 0:HV]))
            chain(V.bn_stats(stw[:, 6:12], win_sb[:, HV:VOCAB]))
            chain(V.bn_aggr(mvw, stw))
            V.tensor_scalar(win_sb, win_sb, mvw[:, 0:1], None, ALU.subtract).then_inc(s_winc, 1)
            dve.wait_ge(s_idx, 16)
            for k in range(ORDER):
                V.tensor_scalar(idx_sb[:, :, k], idx_sb[:, :, k], float(k * (VOCAB + 1)), None, ALU.add).then_inc(s_idx2, 1)
            dve.wait_ge(s_const, 2)
            V.tensor_copy(lnlb, pcol("lnl_b").to_broadcast([P, P])).then_inc(s_dv, 2)
            dve.wait_ge(s_bpp, 1)
            V.tensor_scalar(bp4, TC[:, 0:1], 0.25, None, ALU.mult).then_inc(s_bp, 1)
            for m, pos in ((bmask, lambda q, j: q + 3 * j), (smask, lambda q, j: 3 * q + j)):
                for q in range(3):
                    c = lambda j: ident[:, pos(q, j):pos(q, j) + 1]
                    chain(V.tensor_tensor(m[:, q:q + 1], c(0), c(1), ALU.add))
                    chain(V.tensor_tensor(m[:, q:q + 1], m[:, q:q + 1], c(2), ALU.add))
            dve.wait_ge(s_bf, 16)
            for q in range(3):
                chain(V.tensor_copy(bh, bfs))
                if q == 0:
                    chain(V.tensor_scalar(bias_parts[:, :], bh, bmask[:, 0:1], None, ALU.mult))
                else:
                    chain(V.scalar_tensor_tensor(out=bias_parts[:, :], in0=bh, scalar=bmask[:, q:q + 1], in1=bias_parts[:, :],
                                                 op0=ALU.mult, op1=ALU.add))
                if q < 2:
                    chain(V.tensor_tensor(bfs, bfs, bh, ALU.subtract))
            dve.wait_ge(s_b1m, 1)
            chain(V.tensor_tensor(b1p[:, :], FO[:, 0:DEPTH * FC], pcol("b1", 0, DEPTH * FC), ALU.add))
            for L in range(DEPTH):
                chain(V.tensor_scalar(w1f[:, DFF * L:DFF * L + DFF], w1f[:, DFF * L:DFF * L + DFF], pcol("ln2_w", L), None, ALU.mult))
            V.tensor_reduce(wmaxp[:, 1:2], w1f, AX.X, ALU.max, apply_absolute_value=True).then_inc(s_max, 1)
            dve.wait_ge(s_bom, 1)
            dve.wait_ge(s_bo, 16)
            chain(V.tensor_tensor(bo_row[:, :], bo_row[:, :], FW[:, :], ALU.add))
            chain(V.tensor_scalar(wof, wof, pcol("lnl_w"), None, ALU.mult))
            V.tensor_reduce(wmaxp[:, 2:3], wof, AX.X, ALU.max, apply_absolute_value=True).then_inc(s_max, 1)

            def scale(n):
                if n > 0:
                    dve.wait_ge(s_red, n)
                chain(V.tensor_scalar(wmax[:, n:n + 1], wmax[:, n:n + 1], 1e-30, None, ALU.max))
                chain(V.tensor_scalar(wds[:, n:n + 1], wmax[:, n:n + 1], 1.0 / (WUP * ZUP), None, ALU.mult))
                chain(V.reciprocal(wsc[:, n:n + 1], wmax[:, n:n + 1]))
                chain(V.tensor_scalar(wsc[:, n:n + 1], wsc[:, n:n + 1], WUP, None, ALU.mult))
                V.nop().then_inc(s_scaled, 1)

            chain(V.tensor_tensor(lw, pcol("coeffs", 0, 2), pcol("scales", 0, 2), ALU.mult))
            dve.wait_ge(s_pmag, 1)
            chain(V.tensor_scalar(inv, mag, 1e-30, None, ALU.max))
            chain(V.reciprocal(t3, inv))
            chain(V.tensor_scalar(inv, mag, 0.0, None, ALU.is_equal))
            chain(V.tensor_tensor(t1, pcol("phz_re", 0, 4), t3, ALU.mult))
            chain(V.tensor_tensor(cs1, t1, inv, ALU.add))
            chain(V.tensor_tensor(sn1, pcol("phz_im", 0, 4), t3, ALU.mult))
            chain(V.tensor_tensor(t1, cs1, cs1, ALU.mult))
            chain(V.tensor_tensor(t2, sn1, sn1, ALU.mult))
            chain(V.tensor_tensor(t3, t1, t2, ALU.add))
            chain(V.tensor_scalar(t3, t3, -0.5, 1.5, ALU.mult, ALU.add))
            chain(V.tensor_tensor(cm, cs1, t3, ALU.mult))
            chain(V.tensor_tensor(sm_, sn1, t3, ALU.mult))
            chain(V.tensor_tensor(t1, cm, pcol("lc_re", 0, 4), ALU.mult))
            chain(V.tensor_tensor(t2, sm_, pcol("lc_im", 0, 4), ALU.mult))
            chain(V.tensor_tensor(u0r, t1, t2, ALU.subtract))
            chain(V.tensor_tensor(t1, sm_, pcol("lc_re", 0, 4), ALU.mult))
            chain(V.tensor_tensor(t2, cm, pcol("lc_im", 0, 4), ALU.mult))
            chain(V.tensor_tensor(t3, t1, t2, ALU.add))
            chain(V.tensor_scalar(u0i, t3, -1.0, None, ALU.mult))
            chain(V.memset(cosT[:, :, 0:1], 1.0))
            chain(V.memset(sinT[:, :, 0:1], 0.0))
            m = 1
            while m < SEQ:
                c4 = cm.rearrange("p (l o) -> p l o", o=1).to_broadcast([P, DEPTH, m])
                s4 = sm_.rearrange("p (l o) -> p l o", o=1).to_broadcast([P, DEPTH, m])
                C0, S0 = cosT[:, :, 0:m], sinT[:, :, 0:m]
                chain(V.tensor_tensor(tmp[0][:, :, 0:m], C0, c4, ALU.mult))
                chain(V.tensor_tensor(tmp[1][:, :, 0:m], S0, s4, ALU.mult))
                chain(V.tensor_tensor(cosT[:, :, m:2 * m], tmp[0][:, :, 0:m], tmp[1][:, :, 0:m], ALU.subtract))
                chain(V.tensor_tensor(tmp[0][:, :, 0:m], S0, c4, ALU.mult))
                chain(V.tensor_tensor(tmp[1][:, :, 0:m], C0, s4, ALU.mult))
                chain(V.tensor_tensor(sinT[:, :, m:2 * m], tmp[0][:, :, 0:m], tmp[1][:, :, 0:m], ALU.add))
                chain(V.tensor_tensor(t1, cm, cm, ALU.mult))
                chain(V.tensor_tensor(t2, sm_, sm_, ALU.mult))
                chain(V.tensor_tensor(t3, cm, sm_, ALU.mult))
                chain(V.tensor_tensor(cs1, t1, t2, ALU.subtract))
                chain(V.tensor_tensor(sn1, t1, t2, ALU.add))
                chain(V.tensor_scalar(sn1, sn1, -1.0, 2.0, ALU.mult, ALU.add))
                chain(V.tensor_tensor(cm, cs1, sn1, ALU.mult))
                chain(V.tensor_scalar(t3, t3, 2.0, None, ALU.mult))
                chain(V.tensor_tensor(sm_, t3, sn1, ALU.mult))
                m *= 2
            dve.wait_ge(s_rad, 1)
            dve.wait_ge(s_rows, 16)

            def norm_stats(n, src, tiles, width, s_stat, s_mean, v):
                parts = max(1, width // 512)
                for t in range(tiles):
                    for q in range(parts):
                        w = width // parts
                        last = V.bn_stats(st[n][:, t, 6 * q:6 * q + 6], src(t)[:, q * w:q * w + w])
                last.then_inc(s_stat, 1)
                done_v = held(dve, v + 1)
                dve.wait_ge(s_const, 2)
                dve.wait_ge(s_stat, done_v)
                for t in range(tiles):
                    last = V.bn_aggr(mv[n][:, t, :], st[n][:, t, 0:6 * parts])
                last.then_inc(s_mean, 1)

            def normalise(n, dst, hs):
                for t in range(TPS):
                    last = V.tensor_scalar(dst[:, P * t:P * t + P], hs(t), mv[n][:, t, 0:1], rs[n][:, t:t + 1],
                                           ALU.subtract, ALU.mult)
                return last

            def tile_stats(slot, tau):
                if isinstance(tau, int) and tau < STEPS:
                    dve.wait_ge(s_fT[tau // TPS], 16 * TPS * ORDER)
                else:
                    dve.wait_ge(s_gT, 64 * (tau - STEPS) + 64)
                for q in range(2):
                    last = V.bn_stats(st["i"][:, slot, 6 * q:6 * q + 6], G[:, slot, q * HV:q * HV + HV])
                last.then_inc(i_st, 1)
                done_v = held(dve, tau + 1)
                dve.wait_ge(s_const, 2)
                dve.wait_ge(i_st, done_v)
                V.bn_aggr(mv["i"][:, slot, :], st["i"][:, slot, :]).then_inc(i_mv, 1)

            for t in range(TPS):
                tile_stats(t, t)
            for n in (1, 2):
                scale(n)
            dve.wait_ge(s_hi, 1)
            V.scalar_tensor_tensor(out=w1l[:, :], in0=w1f, scalar=wsc[:, 1:2], in1=w1h[:, :], op0=ALU.mult, op1=ALU.subtract).then_inc(s_lo, 1)
            dve.wait_ge(s_hi, 2)
            V.scalar_tensor_tensor(out=wol[:, :], in0=wof, scalar=wsc[:, 2:3], in1=woh[:, :], op0=ALU.mult, op1=ALU.subtract).then_inc(s_lo, 1)
            for b in range(2):
                dve.wait_ge(s_ptd[b], 64)
            dve.wait_ge(s_ptl, 16)

            def body(r):
                p = r.p
                for k in range(r.steps()):
                    u, uf, tau, L, Lf = STEPS * p + k, STEPS * p + k - 1, STEPS * (p - 1) + k, k // 2, (k - 1) % STEPS // 2
                    layers, ffn, end = r.layers, r.ffn(k), r.end(k)
                    hc, hf = h[k % 2], h[(k - 1) % 2]
                    flat = lambda a: a[:, :, :].rearrange("p t d -> p (t d)")
                    if r.first and k == 1:
                        for t in range(TPS, STEPS):
                            tile_stats(t, t)
                    def stats_conv():
                        if k < 2:
                            dve.wait_ge(i_h, 2 * p + k + 1)
                        else:
                            dve.wait_ge(f_h, u - 1)
                        norm_stats("c", lambda t: hc[:, t, :], TPS, DIM, c_st, c_mv, u)

                    def stats_ffn(v=uf, hs=hf):
                        dve.wait_ge(c_h, v + 1)
                        norm_stats("f", lambda t: hs[:, t, :], TPS, DIM, f_st, f_mv, v)

                    def stats_last():
                        dve.wait_ge(f_h, u - 1)
                        norm_stats("l", lambda t: fy[:, P * t:P * t + P], TPS, DIM, l_st, l_mv, 2 * (p - 1) + k)

                    def z_conv():
                        dve.wait_ge(c_rs, u + 1)
                        after(dve, c_zT, u)
                        normalise("c", cz, lambda t: hc[:, t, :]).then_inc(c_z, 1)

                    def z_ffn():
                        dve.wait_ge(f_rs, uf + 1)
                        after(dve, f_zT, uf)
                        normalise("f", fz, lambda t: hf[:, t, :]).then_inc(f_z, 1)

                    def low_halves(f, l):
                        if f and ffn:
                            dve.wait_ge(f_zh, uf + 1)
                            after(dve, f_f1, 4 * uf)
                            V.scalar_tensor_tensor(out=fzl[:, :], in0=TF[:, :], scalar=ZUP, in1=fzh[:, :],
                                                   op0=ALU.mult, op1=ALU.subtract).then_inc(f_zl, 1)
                        if l and r.last(k):
                            dve.wait_ge(l_zh, 2 * (p - 1) + k + 1)
                            V.scalar_tensor_tensor(out=lzl[k][:, :], in0=TC[:, :], scalar=ZUP, in1=lzh[k][:, :],
                                                   op0=ALU.mult, op1=ALU.subtract).then_inc(l_zl, 1)

                    if r.ffn_first(k):
                        z_ffn()
                    if layers and k < 2:
                        v = 2 * p + k
                        if r.first:
                            dve.wait_ge(s_fP[k], 16 * TPS * ORDER)
                        else:
                            dve.wait_ge(s_gP, 64 * (TPS * v + TPS - STEPS))
                        dve.wait_ge(i_rs, TPS * v + TPS)
                        after(dve, f_h, u - 1)
                        for t in range(TPS):
                            slot = TPS * k + t
                            last = V.scalar_tensor_tensor(out=hc[:, t, :], in0=pacc[:, slot, :], scalar=rs["i"][:, slot:slot + 1],
                                                          in1=bin_row[:, :], op0=ALU.mult, op1=ALU.add)
                        last.then_inc(i_h, 1)
                    if layers:
                        stats_conv()
                    if r.ffn_first(k):
                        low_halves(True, False)
                        z_conv()
                        stats_last()
                    else:
                        if ffn:
                            stats_ffn()
                        if r.last(k):
                            stats_last()
                        if layers:
                            z_conv()
                        if ffn:
                            z_ffn()
                    if r.last(k):
                        dve.wait_ge(l_rs, 2 * (p - 1) + k + 1)
                        V.scalar_tensor_tensor(out=nm[:, :], in0=mv["l"][:, :, 0], scalar=-1.0, in1=rs["l"][:, :],
                                               op0=ALU.mult, op1=ALU.mult).then_inc(l_nm, 1)

                    if r.end_late(k):
                        te = tau - 2
                        dve.wait_ge(e_mm, 2 * te + 2)
                        after(dve, s_out_b, 16 * te)
                        V.scalar_tensor_tensor(out=oh[:, :], in0=FO[:, HV:VOCAB], scalar=wds[:, 0:1], in1=h2[k % 2][:, HV:VOCAB],
                                               op0=ALU.mult, op1=ALU.add).then_inc(e_out, 1)

                    def end_sum():
                        dve.wait_ge(e_wo, tau + 1)
                        if not (r.n == 1 and k < 2):
                            dve.wait_ge(s_out[k % 2], 16 * ((STEPS // 2) * (p - 1) + k // 2))
                            dve.wait_ge(e_out, 2 * tau - 2)
                        dve.wait_ge(s_mv, tau + 1)
                        V.scalar_tensor_tensor(out=h2[k % 2], in0=FW[:, :], scalar=wds[:, 2:3], in1=H1[:, k, :],
                                               op0=ALU.mult, op1=ALU.add).then_inc(e_h2, 1)
                        dve.wait_ge(e_h2, tau + 1)
                        norm_stats("e", lambda t: h2[k % 2], 1, VOCAB, e_st, e_mv, tau)

                    def end_z():
                        dve.wait_ge(e_rs, tau + 1)
                        after(dve, e_T, tau)
                        V.tensor_scalar(ez, h2[k % 2], mv["e"][:, 0, 0:1], rs["e"][:, 0:1], ALU.subtract, ALU.mult).then_inc(e_z, 1)

                    def end_low():
                        dve.wait_ge(e_zh, tau + 1)
                        V.scalar_tensor_tensor(out=ezT[k % 2][:, 1, :], in0=FW[:, :], scalar=ZUP, in1=ezT[k % 2][:, 0, :],
                                               op0=ALU.mult, op1=ALU.subtract).then_inc(e_zl, 1)

                    def move():
                        if r.first and k == STEPS - 1:
                            dve.wait_ge(s_wlo, VC)
                        V.tensor_tensor(H1[:, k, :], G[:, k, :], bo_row[:, :], ALU.add).then_inc(s_mv, 1)

                    def scans():
                        rb = rad[:, L:L + 1].to_broadcast([P, SEQ])
                        for n, (src, dst, u0) in enumerate(((cxc, cur, u0r), (cxs, cui, u0i))):
                            dve.wait_ge(c_rot, 2 * u + n + 1)
                            V.tensor_tensor_scan(dst, rb, src, u0[:, L:L + 1], ALU.mult, ALU.add).then_inc(c_scan, 1)

                    def back():
                        for n, (src, dst, tab) in enumerate(((cur, cxc, cosT), (cui, cxs, sinT))):
                            dve.wait_ge(c_scan, 2 * u + n + 1)
                            V.scalar_tensor_tensor(out=dst, in0=src, scalar=pcol("sc_lin", L), in1=tab[:, L, :],
                                                   op0=ALU.mult, op1=ALU.mult).then_inc(c_prod, 1)
                        dve.wait_ge(c_prod, 2 * u + 2)
                        V.tensor_tensor(cy, cxc, cxs, ALU.add).then_inc(c_y, 1)

                    def lora_sum(v):
                        dve.wait_ge(s_weff, 16 * VC // 2)
                        dve.wait_ge(s_lom, v + 1)
                        after(dve, s_wlo, v - 1)
                        V.tensor_tensor(wsum[v % 2], weff[:, v, :], FO[:, :], ALU.add).then_inc(s_lad, 1)

                    def lora_low(v):
                        dve.wait_ge(s_whi, v + 1)
                        V.scalar_tensor_tensor(out=we[:, v, 1, :], in0=wsum[v % 2], scalar=wsc[:, 0:1], in1=we[:, v, 0, :],
                                               op0=ALU.mult, op1=ALU.subtract).then_inc(s_wlo, 1)

                    def largest():
                        if k == 0:
                            dve.wait_ge(s_lora, 16 * (1 + KC))
                            for q in range(KC):
                                chain(V.tensor_scalar(lb[q], lb[q], lw[:, q:q + 1], None, ALU.mult))
                            V.nop().then_inc(s_lbs, 1)
                            chain(V.tensor_reduce(dmaxp[:, 1:2], la, AX.XY, ALU.max, apply_absolute_value=True))
                            for q in range(KC):
                                chain(V.tensor_reduce(wpart[:, q:q + 1], lb[q], AX.X, ALU.max, apply_absolute_value=True))
                            chain(V.tensor_tensor(dmaxp[:, 2:3], wpart[:, 0:1], wpart[:, 1:2], ALU.max))
                        else:
                            dve.wait_ge(s_weff, 16 * VC // 2)
                            for q in (2 * k - 2, 2 * k - 1):
                                chain(V.tensor_reduce(wpart[:, q:q + 1], weff[:, 2 * q:2 * q + 2, :], AX.XY, ALU.max, apply_absolute_value=True))
                        if k == 2:
                            V.tensor_reduce(dmaxp[:, 0:1], wpart, AX.X, ALU.max, apply_absolute_value=True).then_inc(s_max, 1)

                    def dense_scale():
                        dve.wait_ge(s_red, 3)
                        chain(V.tensor_tensor(t1[:, 0:1], dmax[:, 1:2], dmax[:, 2:3], ALU.mult))
                        chain(V.scalar_tensor_tensor(out=wmax[:, 0:1], in0=t1[:, 0:1], scalar=float(EXP), in1=dmax[:, 0:1], op0=ALU.mult, op1=ALU.add))
                        scale(0)
                        b3 = sparts[:, 3:4].bitcast(bf16)[:, 0:1]
                        chain(V.tensor_scalar(sparts[:, 0:1], wsc[:, 0:1], ZUP, None, ALU.mult))
                        for q in range(3):
                            chain(V.tensor_copy(b3, sparts[:, 0:1]))
                            if q == 0:
                                chain(V.tensor_tensor(sparts[:, 1:2], b3, smask[:, 0:1], ALU.mult))
                            else:
                                chain(V.tensor_tensor(sparts[:, 2:3], b3, smask[:, q:q + 1], ALU.mult))
                                chain(V.tensor_tensor(sparts[:, 1:2], sparts[:, 1:2], sparts[:, 2:3], ALU.add))
                            if q < 2:
                                chain(V.tensor_tensor(sparts[:, 0:1], sparts[:, 0:1], b3, ALU.subtract))
                        chain(V.tensor_copy(sc_parts[:, :], sparts[:, 1:2].to_broadcast([P, P])))

                    def out_half():
                        tp = tau - 1
                        dve.wait_ge(e_mm, 2 * tp + 1)
                        hb = h2[(k - 1) % 2][:, 0:HV]
                        V.scalar_tensor_tensor(out=hb, in0=FO[:, 0:HV], scalar=wds[:, 0:1], in1=hb, op0=ALU.mult, op1=ALU.add).then_inc(e_out, 1)

                    def conv_sum():
                        dve.wait_ge(c_yT, u + 1)
                        V.tensor_tensor(flat(hc), flat(hc), TC[:, :], ALU.add).then_inc(c_h, 1)

                    def ffn_sum():
                        dve.wait_ge(f_yT, uf + 1)
                        V.tensor_tensor(fy[:, :] if Lf == DEPTH - 1 else flat(hf), flat(hf), TF[:, :], ALU.add).then_inc(f_h, 1)

                    if end and k == 0:
                        low_halves(True, False)
                        if layers:
                            scans()
                        if layers:
                            back()
                        low_halves(False, True)
                        if r.end_mm(k):
                            out_half()
                        for n in r.stats_at(k)[:1]:
                            tile_stats((6 + n) % STEPS, STEPS * p + 6 + n)
                        end_sum()
                        if layers:
                            move()
                        end_z()
                        if layers:
                            conv_sum()
                        if ffn:
                            ffn_sum()
                        if r.ffn_first(k + 1):
                            stats_ffn(u, hc)
                        end_low()
                        for n in r.stats_at(k)[1:]:
                            tile_stats((6 + n) % STEPS, STEPS * p + 6 + n)
                    else:
                        if end:
                            end_sum()
                        split = r.lora(k - 1) if k > 0 else None
                        if split is not None:
                            lora_sum(split + 1)
                        if not r.ffn_first(k):
                            low_halves(True, True)
                        if split is not None:
                            lora_low(split)
                            lora_low(split + 1)
                        if layers:
                            move()
                            scans()
                        if end:
                            end_z()
                        if r.ffn_first(k):
                            low_halves(False, True)
                        if layers:
                            back()
                        for n in r.stats_at(k):
                            tile_stats((6 + n) % STEPS, STEPS * p + 6 + n)
                        if end:
                            end_low()
                        if r.end_mm(k):
                            out_half()
                        if layers:
                            conv_sum()
                        if r.first and k == 3:
                            dense_scale()
                        if r.lora(k) is not None:
                            lora_sum(r.lora(k))
                        if ffn:
                            ffn_sum()
                        if r.first and k < 3:
                            largest()
            rounds(dve, body)


def kernel(x, L0_tok_W, L0_tok_b, L0_attn_Win, L0_attn_bin, L0_attn_ln1_w, L0_attn_ln1_b, L0_attn_phz_re,
           L0_attn_phz_im, L0_attn_lc_re, L0_attn_lc_im, L0_attn_sc_lin, L0_attn_ln2_w, L0_attn_ln2_b, L0_attn_W1,
           L0_attn_b1, L0_attn_W2, L0_attn_b2, L0_attn_lnl_w, L0_attn_lnl_b, L0_attn_Wout, L0_attn_bout, L0_ffn_W,
           L0_ffn_bias, L0_ffn_A, L0_ffn_Bf, L0_ffn_coeffs, L0_ffn_scales):
    import numpy as np
    import concourse.bacc as bacc
    from concourse.bass_utils import run_bass_kernel_spmd

    a = lambda v: np.asarray(v)
    c = np.ascontiguousarray
    xs = a(x)
    ctxs = np.stack([np.pad(xs, ((0, 0), (s, 0)), constant_values=VOCAB)[:, :SEQ] for s in range(ORDER - 1, -1, -1)], -1)
    idx = c(ctxs.reshape(TILES, P, ORDER).transpose(1, 0, 2))
    per_ch = lambda v, n: a(v).reshape(n, P).T
    parts = {
        "ln1_w": per_ch(L0_attn_ln1_w, 4), "ln1_b": per_ch(L0_attn_ln1_b, 4), "phz_re": per_ch(L0_attn_phz_re, 4),
        "phz_im": per_ch(L0_attn_phz_im, 4), "lc_re": per_ch(L0_attn_lc_re, 4), "lc_im": per_ch(L0_attn_lc_im, 4),
        "sc_lin": per_ch(L0_attn_sc_lin, 4), "ln2_w": per_ch(L0_attn_ln2_w, 4), "ln2_b": per_ch(L0_attn_ln2_b, 4),
        "b2": per_ch(L0_attn_b2, 4), "b1": per_ch(L0_attn_b1, 16), "lnl_w": per_ch(L0_attn_lnl_w, 1),
        "lnl_b": per_ch(L0_attn_lnl_b, 1), "tok_b": per_ch(L0_tok_b, 8),
        "coeffs": np.repeat(a(L0_ffn_coeffs), 16).reshape(2, P).T, "scales": np.repeat(a(L0_ffn_scales), 16).reshape(2, P).T,
    }
    cols = c(np.concatenate([parts[n] for n in PCOLS], 1))
    chunks = lambda m: c(m.reshape(-1, P, m.shape[-1]).transpose(1, 0, 2))
    W1 = a(L0_attn_W1)
    arrays = {
        "idx": idx, "tok_wt": c(a(L0_tok_W).T), "tok_w": c(a(L0_tok_W)), "cols": cols, "tok_b": c(a(L0_tok_b)),
        "win": c(a(L0_attn_Win)), "bin": c(a(L0_attn_bin)),
        "w1t": c(W1.transpose(2, 0, 1).reshape(P, DEPTH * DFF)),
        "w2t": c(a(L0_attn_W2).transpose(0, 2, 1).reshape(DEPTH, DFF // P, P, DIM).transpose(2, 0, 1, 3)),
        "woutt": c(a(L0_attn_Wout).T), "bout": c(a(L0_attn_bout)), "ffn_wt": chunks(a(L0_ffn_W).T), "ffn_bias": c(a(L0_ffn_bias)),
        "lora_a": chunks(a(L0_ffn_A).reshape(EXP, VOCAB)),
        "lora_bt": chunks(c(a(L0_ffn_Bf).transpose(0, 2, 1)).reshape(EXP, VOCAB)),
    }
    nc = bacc.Bacc("TRN2", target_bir_lowering=False, num_devices=1)
    args = [nc.dram_tensor(n, v.shape, mybir.dt.from_np(v.dtype), kind="ExternalInput").ap() for n, v in arrays.items()]
    out = nc.dram_tensor("out", (NSEQ * SEQ, VOCAB), mybir.dt.float32, kind="ExternalOutput").ap()
    ptab = nc.dram_tensor("ptab", (ROWS, DIM), mybir.dt.float32, kind="Internal").ap()
    program(nc, *args, out, ptab)
    r = run_bass_kernel_spmd(nc, [arrays], core_ids=[0])
    return r.results[0]["out"].reshape(NSEQ, SEQ, VOCAB)
```
